# Optimizing a Trainium2 kernel written in Bass

```python
import numpy as np
import jax
import jax.numpy as jnp

def _softmax(x, axis=-1):
    return jax.nn.softmax(x, axis=axis)

def _gelu(x):
    return jax.nn.gelu(x, approximate=True)

def _silu(x):
    return jax.nn.silu(x)

def _sigmoid(x):
    return jax.nn.sigmoid(x)

def _layernorm(x, axis=-1, eps=1e-05):
    m = jnp.mean(x, axis=axis, keepdims=True)
    v = jnp.var(x, axis=axis, keepdims=True)
    return (x - m) / jnp.sqrt(v + eps)

def _scatter_add(tgt, idx, src, axis=0):
    return tgt.at[idx].add(src)

def _segment_sum(src, seg, n):
    return jax.ops.segment_sum(src, seg, n)
kernel_name = 'mk_xattn_ffn_d4_seqx_r8_d3921a'

def setup_inputs(seed: int=0):
    np.random.seed(seed)
    _w = jnp.asarray

    def _rec_inputs():
        import jax
        import jax.numpy as jnp
        _rk = jax.random.key(seed)
        x = -0.0003929 + 0.9999 * jax.random.normal(jax.random.fold_in(_rk, 1), (16, 64, 256), jnp.float32)
        _lenS = 64 - jax.random.randint(jax.random.fold_in(_rk, 7), (16,), 0, max(1, 64 // 4) + 1, jnp.int32)
        _lenS2 = 64 - jax.random.randint(jax.random.fold_in(_rk, 8), (16,), 0, max(1, 64 // 4) + 1, jnp.int32)
        _ctx_2048P = jax.random.normal(jax.random.fold_in(_rk, 11), (16, 16, 256), jnp.float32)
        _ctx_2048c = jax.random.dirichlet(jax.random.fold_in(_rk, 511), 0.3 * jnp.ones((16,), jnp.float32), (16, 64))
        _ctx_2048t = jnp.einsum('bsk,bkd->bsd', _ctx_2048c, _ctx_2048P)
        _ctx_2048t = _ctx_2048t * jax.lax.rsqrt(jnp.mean(jnp.square(_ctx_2048t)) + 1e-12) * 0.953939
        ctx_2048 = -0.000514642 + 1.00011 * (_ctx_2048t + 0.3 * jax.random.normal(jax.random.fold_in(_rk, 611), (16, 64, 256), jnp.float32))
        return (x, ctx_2048)
    x, ctx_2048 = _rec_inputs()

    def _L0_xattn_setup():
        import jax, jax.numpy as jnp
        import numpy as np
        NUM_HEADS = 16

        def _qdq(x):
            s = jnp.maximum(jnp.max(jnp.abs(x), axis=-1, keepdims=True) / 127.0, 1e-08)
            return jnp.clip(jnp.round(x / s), -127.0, 127.0) * s
        key = jax.random.key(seed)
        ks = jax.random.split(key, 8)
        B, N, M, D = (2, 512, 64, 256)
        w_std = 0.02
        return {'x': jax.random.normal(ks[0], (B, N, D), jnp.float32), 'cond': jax.random.normal(ks[1], (B, M, D), jnp.float32), 'wq': jax.random.normal(ks[2], (D, D), jnp.float32) * w_std, 'bq': jax.random.normal(ks[3], (D,), jnp.float32) * w_std, 'wkv': jax.random.normal(ks[4], (2 * D, D), jnp.float32) * w_std, 'bkv': jax.random.normal(ks[5], (2 * D,), jnp.float32) * w_std, 'wp': jax.random.normal(ks[6], (D, D), jnp.float32) * w_std, 'bp': jax.random.normal(ks[7], (D,), jnp.float32) * w_std}
    _L0_xattn_all = _L0_xattn_setup()
    _L0_xattn_in = {k: v for k, v in _L0_xattn_all.items() if k in ('wq', 'bq', 'wkv', 'bkv', 'wp', 'bp')}
    del _L0_xattn_all

    def _L0_ffn_setup():
        import jax, jax.numpy as jnp
        import numpy as np
        N_EXPERTS = 8
        TOP_K = 2
        N_GROUP = 4
        TOPK_GROUP = 2
        ROUTED_SCALE = 1.0

        def _group_limited_topk(scores):
            T, N = scores.shape
            E = N // N_GROUP
            group_scores = scores.reshape(T, N_GROUP, E).max(axis=-1)
            _, gidx = jax.lax.top_k(group_scores, TOPK_GROUP)
            gmask = jax.nn.one_hot(gidx, N_GROUP, dtype=scores.dtype).sum(1)
            smask = jnp.repeat(gmask, E, axis=1)
            masked = jnp.where(smask > 0, scores, jnp.zeros((), scores.dtype))
            topk_w, topk_i = jax.lax.top_k(masked, TOP_K)
            return (topk_w, topk_i)
        key = jax.random.key(seed)
        ks = jax.random.split(key, 8)
        B, S, H, F, FS, N = (2, 128, 256, 176, 352, N_EXPERTS)
        std = jnp.float32(0.02)
        return {'hidden_states': jax.random.normal(ks[0], (B, S, H), jnp.float32), 'gate_weight': jax.random.normal(ks[1], (N, H), jnp.float32) * std, 'gate_w': jax.random.normal(ks[2], (N, F, H), jnp.float32) * std, 'up_w': jax.random.normal(ks[3], (N, F, H), jnp.float32) * std, 'down_w': jax.random.normal(ks[4], (N, H, F), jnp.float32) * std, 'sh_gate_w': jax.random.normal(ks[5], (FS, H), jnp.float32) * std, 'sh_up_w': jax.random.normal(ks[6], (FS, H), jnp.float32) * std, 'sh_down_w': jax.random.normal(ks[7], (H, FS), jnp.float32) * std}
    _L0_ffn_all = _L0_ffn_setup()
    _L0_ffn_in = {k: v for k, v in _L0_ffn_all.items() if k in ('gate_weight', 'gate_w', 'up_w', 'down_w', 'sh_gate_w', 'sh_up_w', 'sh_down_w')}
    del _L0_ffn_all

    def _L1_xattn_setup():
        import jax, jax.numpy as jnp
        import numpy as np
        B, S, D = (8, 128, 256)
        H, HD = (16, 128)
        key = jax.random.key(seed)
        ks = jax.random.split(key, 6)
        fan_in = 1.0 / np.sqrt(D)
        return {'inputs_q': jax.random.normal(ks[0], (B, S, D), jnp.float32), 'inputs_kv': jax.random.normal(ks[1], (B, S, D), jnp.float32), 'Wq': jax.random.normal(ks[2], (D, H * HD), jnp.float32) * fan_in, 'Wk': jax.random.normal(ks[3], (D, H * HD), jnp.float32) * fan_in, 'Wv': jax.random.normal(ks[4], (D, H * HD), jnp.float32) * fan_in, 'Wo': jax.random.normal(ks[5], (H * HD, D), jnp.float32) * (1.0 / np.sqrt(H * HD))}
    _L1_xattn_all = _L1_xattn_setup()
    _L1_xattn_in = {k: v for k, v in _L1_xattn_all.items() if k in ('Wq', 'Wk', 'Wv', 'Wo')}
    del _L1_xattn_all

    def _L1_ffn_setup():
        import jax, jax.numpy as jnp
        import numpy as np
        K = 2
        SCALING = 16.0 / 16.0
        key = jax.random.key(seed)
        ks = jax.random.split(key, 7)
        B, T, D, O, E, R = (2, 512, 256, 256, 8, 16)
        return {'x': jax.random.normal(ks[0], (B, T, D), dtype=jnp.float32), 'W': jax.random.normal(ks[1], (O, D), dtype=jnp.float32) * (1.0 / np.sqrt(D)), 'b': jax.random.normal(ks[2], (O,), dtype=jnp.float32) * 0.02, 'lora_A': jax.random.normal(ks[3], (E, R, D), dtype=jnp.float32) * (1.0 / np.sqrt(D)), 'lora_B': jax.random.normal(ks[4], (E, O, R), dtype=jnp.float32) * 0.02, 'gate_w': jax.random.normal(ks[5], (E, D), dtype=jnp.float32) * 0.02, 'gate_b': jax.random.normal(ks[6], (E,), dtype=jnp.float32) * 0.02}
    _L1_ffn_all = _L1_ffn_setup()
    _L1_ffn_in = {k: v for k, v in _L1_ffn_all.items() if k in ('W', 'b', 'lora_A', 'lora_B', 'gate_w', 'gate_b')}
    del _L1_ffn_all

    def _L2_xattn_setup():
        import jax, jax.numpy as jnp
        import numpy as np
        B, S, DIM, HD = (4, 128, 256, 128)
        H = DIM // HD
        GN_EPS = 0.001

        def _decay_masks(n_heads, seq_len):
            gam = 1.0 - 2.0 ** (-5.0 - jnp.arange(n_heads, dtype=jnp.float32))
            idx = jnp.arange(seq_len, dtype=jnp.float32)
            expo = idx[None, :] - idx[:, None]
            D = jnp.where(expo[None, :, :] <= 0, gam[:, None, None] ** expo[None, :, :], 0.0)
            return D / jnp.sqrt(D.sum(axis=-1))[:, None, :]
        key = jax.random.key(seed)
        ks = jax.random.split(key, 8)
        x = jax.random.normal(ks[0], (B, S, DIM), dtype=jnp.float32)
        k = jax.random.normal(ks[1], (B, S, DIM), dtype=jnp.float32)
        v = jax.random.normal(ks[2], (B, S, DIM), dtype=jnp.float32)
        Wh = jax.random.normal(ks[3], (H, HD, HD), dtype=jnp.float32) / np.sqrt(HD)
        wg_w = jax.random.normal(ks[4], (DIM, DIM), dtype=jnp.float32) / np.sqrt(DIM)
        wo_w = jax.random.normal(ks[5], (DIM, DIM), dtype=jnp.float32) / np.sqrt(DIM)
        gn_gamma = jnp.ones((DIM,), dtype=jnp.float32)
        gn_beta = jnp.zeros((DIM,), dtype=jnp.float32)
        return {'x': x, 'k': k, 'v': v, 'Wh': Wh, 'wg_w': wg_w, 'wo_w': wo_w, 'gn_gamma': gn_gamma, 'gn_beta': gn_beta}
    _L2_xattn_all = _L2_xattn_setup()
    _L2_xattn_in = {k: v for k, v in _L2_xattn_all.items() if k in ('Wh', 'wg_w', 'wo_w', 'gn_gamma', 'gn_beta')}
    del _L2_xattn_all

    def _L2_ffn_setup():
        import jax, jax.numpy as jnp
        import numpy as np
        D_MODEL = 256
        HIDDEN = 704
        NUM_EXPERTS = 8
        TOP_K = 2

        def _moe(x, Wg, W1, W3, W2):
            gate_logits = jnp.einsum('bsd,de->bse', x, Wg)
            gate_weights = jax.nn.softmax(gate_logits, axis=-1)
            topk_w, topk_idx = jax.lax.top_k(gate_weights, TOP_K)
            topk_w = topk_w / jnp.sum(topk_w, axis=-1, keepdims=True)
            combine = jnp.sum(jax.nn.one_hot(topk_idx, NUM_EXPERTS, dtype=x.dtype) * topk_w[..., None], axis=-2)
            out = jnp.zeros_like(x)
            for e in range(NUM_EXPERTS):
                gate = jax.nn.silu(jnp.einsum('bsd,dh->bsh', x, W1[e]))
                val = jnp.einsum('bsd,dh->bsh', x, W3[e])
                y = jnp.einsum('bsh,hd->bsd', gate * val, W2[e])
                out = out + combine[..., e:e + 1] * y
            return out
        key = jax.random.key(seed)
        ks = jax.random.split(key, 5)
        s_in = 1.0 / np.sqrt(D_MODEL)
        s_h = 1.0 / np.sqrt(HIDDEN)
        x = jax.random.normal(ks[0], (4, 128, D_MODEL), dtype=jnp.float32)
        Wg = jax.random.normal(ks[1], (D_MODEL, NUM_EXPERTS), dtype=jnp.float32) * s_in
        W1 = jax.random.normal(ks[2], (NUM_EXPERTS, D_MODEL, HIDDEN), dtype=jnp.float32) * s_in
        W3 = jax.random.normal(ks[3], (NUM_EXPERTS, D_MODEL, HIDDEN), dtype=jnp.float32) * s_in
        W2 = jax.random.normal(ks[4], (NUM_EXPERTS, HIDDEN, D_MODEL), dtype=jnp.float32) * s_h
        return {'x': x, 'Wg': Wg, 'W1': W1, 'W3': W3, 'W2': W2}
    _L2_ffn_all = _L2_ffn_setup()
    _L2_ffn_in = {k: v for k, v in _L2_ffn_all.items() if k in ('Wg', 'W1', 'W3', 'W2')}
    del _L2_ffn_all

    def _L3_xattn_setup():
        import jax, jax.numpy as jnp
        import numpy as np
        N_HEAD = 8
        key = jax.random.key(seed)
        k1, k2, k3 = jax.random.split(key, 3)
        b, d, m = (4, 128, 256)
        c, n = (128, 256)
        q = jax.random.normal(k1, (b, d, m), dtype=jnp.float32)
        k = jax.random.normal(k2, (d // d * b, d, n), dtype=jnp.float32).reshape(b, d, n)
        v = jax.random.normal(k3, (b, c, n), dtype=jnp.float32)
        return {'q': q, 'k': k, 'v': v}
    _L3_xattn_all = _L3_xattn_setup()
    _L3_xattn_in = {k: v for k, v in _L3_xattn_all.items() if k in ()}
    del _L3_xattn_all

    def _L3_ffn_setup():
        import jax, jax.numpy as jnp
        import numpy as np
        HIDDEN = 256
        INTER = 1024
        RETRIEVAL = 128
        NUM_EXPERTS = 512
        NUM_KEYS = 64
        TOP_K = 8
        B, S = (4, 256)
        key = jax.random.key(seed)
        ks = jax.random.split(key, 8)
        sc = 0.02
        return {'hidden_states': jax.random.normal(ks[0], (B, S, HIDDEN), jnp.float32), 'W_q': jax.random.normal(ks[1], (HIDDEN, RETRIEVAL), jnp.float32) * sc, 'keys': jax.random.normal(ks[2], (2, RETRIEVAL // 2, NUM_KEYS), jnp.float32) * sc, 'down_embed': jax.random.normal(ks[3], (NUM_EXPERTS, HIDDEN), jnp.float32) * sc, 'up_embed': jax.random.normal(ks[4], (NUM_EXPERTS, HIDDEN), jnp.float32) * sc, 'gate_w': jax.random.normal(ks[5], (HIDDEN, INTER), jnp.float32) * sc, 'up_w': jax.random.normal(ks[6], (HIDDEN, INTER), jnp.float32) * sc, 'down_w': jax.random.normal(ks[7], (INTER, HIDDEN), jnp.float32) * sc}
    _L3_ffn_all = _L3_ffn_setup()
    _L3_ffn_in = {k: v for k, v in _L3_ffn_all.items() if k in ('W_q', 'keys', 'down_embed', 'up_embed', 'gate_w', 'up_w', 'down_w')}
    del _L3_ffn_all
    return {'x': x, 'ctx_2048': ctx_2048, 'L0_xattn_wq': _L0_xattn_in['wq'], 'L0_xattn_bq': _L0_xattn_in['bq'], 'L0_xattn_wkv': _L0_xattn_in['wkv'], 'L0_xattn_bkv': _L0_xattn_in['bkv'], 'L0_xattn_wp': _L0_xattn_in['wp'], 'L0_xattn_bp': _L0_xattn_in['bp'], 'L0_ffn_gate_weight': _L0_ffn_in['gate_weight'], 'L0_ffn_gate_w': _L0_ffn_in['gate_w'], 'L0_ffn_up_w': _L0_ffn_in['up_w'], 'L0_ffn_down_w': _L0_ffn_in['down_w'], 'L0_ffn_sh_gate_w': _L0_ffn_in['sh_gate_w'], 'L0_ffn_sh_up_w': _L0_ffn_in['sh_up_w'], 'L0_ffn_sh_down_w': _L0_ffn_in['sh_down_w'], 'L1_xattn_Wq': _L1_xattn_in['Wq'], 'L1_xattn_Wk': _L1_xattn_in['Wk'], 'L1_xattn_Wv': _L1_xattn_in['Wv'], 'L1_xattn_Wo': _L1_xattn_in['Wo'], 'L1_ffn_W': _L1_ffn_in['W'], 'L1_ffn_b': _L1_ffn_in['b'], 'L1_ffn_lora_A': _L1_ffn_in['lora_A'], 'L1_ffn_lora_B': _L1_ffn_in['lora_B'], 'L1_ffn_gate_w': _L1_ffn_in['gate_w'], 'L1_ffn_gate_b': _L1_ffn_in['gate_b'], 'L2_xattn_Wh': _L2_xattn_in['Wh'], 'L2_xattn_wg_w': _L2_xattn_in['wg_w'], 'L2_xattn_wo_w': _L2_xattn_in['wo_w'], 'L2_xattn_gn_gamma': _L2_xattn_in['gn_gamma'], 'L2_xattn_gn_beta': _L2_xattn_in['gn_beta'], 'L2_ffn_Wg': _L2_ffn_in['Wg'], 'L2_ffn_W1': _L2_ffn_in['W1'], 'L2_ffn_W3': _L2_ffn_in['W3'], 'L2_ffn_W2': _L2_ffn_in['W2'], 'L3_ffn_W_q': _L3_ffn_in['W_q'], 'L3_ffn_keys': _L3_ffn_in['keys'], 'L3_ffn_down_embed': _L3_ffn_in['down_embed'], 'L3_ffn_up_embed': _L3_ffn_in['up_embed'], 'L3_ffn_gate_w': _L3_ffn_in['gate_w'], 'L3_ffn_up_w': _L3_ffn_in['up_w'], 'L3_ffn_down_w': _L3_ffn_in['down_w']}

def reference(x, ctx_2048, L0_xattn_wq, L0_xattn_bq, L0_xattn_wkv, L0_xattn_bkv, L0_xattn_wp, L0_xattn_bp, L0_ffn_gate_weight, L0_ffn_gate_w, L0_ffn_up_w, L0_ffn_down_w, L0_ffn_sh_gate_w, L0_ffn_sh_up_w, L0_ffn_sh_down_w, L1_xattn_Wq, L1_xattn_Wk, L1_xattn_Wv, L1_xattn_Wo, L1_ffn_W, L1_ffn_b, L1_ffn_lora_A, L1_ffn_lora_B, L1_ffn_gate_w, L1_ffn_gate_b, L2_xattn_Wh, L2_xattn_wg_w, L2_xattn_wo_w, L2_xattn_gn_gamma, L2_xattn_gn_beta, L2_ffn_Wg, L2_ffn_W1, L2_ffn_W3, L2_ffn_W2, L3_ffn_W_q, L3_ffn_keys, L3_ffn_down_embed, L3_ffn_up_embed, L3_ffn_gate_w, L3_ffn_up_w, L3_ffn_down_w):
    import jax
    import jax.numpy as jnp

    def _L0_xattn_ref(x, cond, wq, bq, wkv, bkv, wp, bp):
        import jax, jax.numpy as jnp
        import numpy as np
        NUM_HEADS = 16

        def _qdq(x):
            s = jnp.maximum(jnp.max(jnp.abs(x), axis=-1, keepdims=True) / 127.0, 1e-08)
            return jnp.clip(jnp.round(x / s), -127.0, 127.0) * s
        B, N, C = x.shape
        M = cond.shape[1]
        H = NUM_HEADS
        Dh = C // H
        q = _qdq(x) @ _qdq(wq).T + bq
        kv = cond @ wkv.T + bkv
        k, v = jnp.split(kv, 2, axis=-1)
        q = q.reshape(B, N, H, Dh)
        k = k.reshape(B, M, H, Dh)
        v = v.reshape(B, M, H, Dh)
        scale = 1.0 / np.sqrt(Dh)
        attn = jax.nn.softmax(jnp.einsum('bnhd,bmhd->bhnm', q, k) * scale, axis=-1)
        o = jnp.einsum('bhnm,bmhd->bnhd', attn, v).reshape(B, N, C)
        out = _qdq(o) @ _qdq(wp).T + bp
        return out

    def _L0_ffn_ref(hidden_states, gate_weight, gate_w, up_w, down_w, sh_gate_w, sh_up_w, sh_down_w):
        import jax, jax.numpy as jnp
        import numpy as np
        N_EXPERTS = 8
        TOP_K = 2
        N_GROUP = 4
        TOPK_GROUP = 2
        ROUTED_SCALE = 1.0

        def _group_limited_topk(scores):
            T, N = scores.shape
            E = N // N_GROUP
            group_scores = scores.reshape(T, N_GROUP, E).max(axis=-1)
            _, gidx = jax.lax.top_k(group_scores, TOPK_GROUP)
            gmask = jax.nn.one_hot(gidx, N_GROUP, dtype=scores.dtype).sum(1)
            smask = jnp.repeat(gmask, E, axis=1)
            masked = jnp.where(smask > 0, scores, jnp.zeros((), scores.dtype))
            topk_w, topk_i = jax.lax.top_k(masked, TOP_K)
            return (topk_w, topk_i)
        B, S, H = hidden_states.shape
        h = hidden_states.reshape(-1, H)
        logits = h.astype(jnp.float32) @ gate_weight.astype(jnp.float32).T
        scores = jax.nn.softmax(logits, axis=-1)
        topk_w, topk_i = _group_limited_topk(scores)
        topk_w = (topk_w * ROUTED_SCALE).astype(h.dtype)
        wmat = (jax.nn.one_hot(topk_i, N_EXPERTS, dtype=topk_w.dtype) * topk_w[..., None]).sum(axis=1)
        g = jnp.einsum('th,nfh->ntf', h, gate_w)
        u = jnp.einsum('th,nfh->ntf', h, up_w)
        e = jnp.einsum('ntf,nhf->nth', jax.nn.silu(g) * u, down_w)
        routed = jnp.einsum('nth,tn->th', e, wmat)
        sg = h @ sh_gate_w.T
        su = h @ sh_up_w.T
        shared = jax.nn.silu(sg) * su @ sh_down_w.T
        return (routed + shared).reshape(B, S, H)

    def _L1_xattn_ref(inputs_q, inputs_kv, Wq, Wk, Wv, Wo):
        import jax, jax.numpy as jnp
        import numpy as np
        B, S, D = (8, 128, 256)
        H, HD = (16, 128)
        b, sq, _ = inputs_q.shape
        skv = inputs_kv.shape[1]
        q = (inputs_q @ Wq).reshape(b, sq, H, HD) * (1.0 / np.sqrt(HD))
        k = (inputs_kv @ Wk).reshape(b, skv, H, HD)
        v = (inputs_kv @ Wv).reshape(b, skv, H, HD)
        scores = jnp.einsum('bqhd,bkhd->bhqk', q, k)
        attn = jax.nn.softmax(scores, axis=-1)
        ctx = jnp.einsum('bhqk,bkhd->bqhd', attn, v).reshape(b, sq, H * HD)
        return ctx @ Wo

    def _L1_ffn_ref(x, W, b, lora_A, lora_B, gate_w, gate_b):
        import jax, jax.numpy as jnp
        import numpy as np
        K = 2
        SCALING = 16.0 / 16.0
        orig_shape = x.shape
        D = orig_shape[-1]
        O = W.shape[0]
        x_flat = x.reshape(-1, D)
        base = x_flat @ W.T + b
        logits = x_flat @ gate_w.T + gate_b
        topk_logits, topk_idx = jax.lax.top_k(logits, K)
        gates = jax.nn.softmax(topk_logits, axis=-1)
        xA = jnp.einsum('nd,erd->ner', x_flat, lora_A)
        delta_all = jnp.einsum('ner,eor->neo', xA, lora_B)
        delta_topk = jnp.take_along_axis(delta_all, topk_idx[:, :, None], axis=1)
        lora_update = jnp.sum(delta_topk * gates[:, :, None], axis=1)
        out = base + SCALING * lora_update
        return out.reshape(*orig_shape[:-1], O)

    def _L2_xattn_ref(x, k, v, Wh, wg_w, wo_w, gn_gamma, gn_beta):
        import jax, jax.numpy as jnp
        import numpy as np
        B, S, DIM, HD = (4, 128, 256, 128)
        H = DIM // HD
        GN_EPS = 0.001

        def _decay_masks(n_heads, seq_len):
            gam = 1.0 - 2.0 ** (-5.0 - jnp.arange(n_heads, dtype=jnp.float32))
            idx = jnp.arange(seq_len, dtype=jnp.float32)
            expo = idx[None, :] - idx[:, None]
            D = jnp.where(expo[None, :, :] <= 0, gam[:, None, None] ** expo[None, :, :], 0.0)
            return D / jnp.sqrt(D.sum(axis=-1))[:, None, :]
        b, s, dim = x.shape
        h, hd, _ = Wh.shape
        xh = x.reshape(b, s, h, hd)
        kh = k.reshape(b, s, h, hd)
        vh = v.reshape(b, s, h, hd)
        Q = jnp.einsum('bshd,hde->bshe', xh, Wh)
        K = jnp.einsum('bshd,hde->bshe', kh, Wh)
        V = jnp.einsum('bshd,hde->bshe', vh, Wh)
        scores = jnp.einsum('bshe,bthe->bhst', Q, K) / jnp.sqrt(jnp.float32(hd))
        Dn = _decay_masks(h, s)
        masked = scores * Dn[None, :, :, :]
        A = jnp.maximum(jnp.abs(masked.sum(axis=0)), 1.0)
        O = jnp.einsum('hst,bthe->bshe', A, V).reshape(b, s, dim)
        mu = O.mean(axis=-1, keepdims=True)
        var = O.var(axis=-1, keepdims=True)
        Y = (O - mu) / jnp.sqrt(var + GN_EPS) * gn_gamma + gn_beta
        W = jax.nn.relu(x @ wg_w)
        return W * Y @ wo_w

    def _L2_ffn_ref(x, Wg, W1, W3, W2):
        import jax, jax.numpy as jnp
        import numpy as np
        D_MODEL = 256
        HIDDEN = 704
        NUM_EXPERTS = 8
        TOP_K = 2

        def _moe(x, Wg, W1, W3, W2):
            gate_logits = jnp.einsum('bsd,de->bse', x, Wg)
            gate_weights = jax.nn.softmax(gate_logits, axis=-1)
            topk_w, topk_idx = jax.lax.top_k(gate_weights, TOP_K)
            topk_w = topk_w / jnp.sum(topk_w, axis=-1, keepdims=True)
            combine = jnp.sum(jax.nn.one_hot(topk_idx, NUM_EXPERTS, dtype=x.dtype) * topk_w[..., None], axis=-2)
            out = jnp.zeros_like(x)
            for e in range(NUM_EXPERTS):
                gate = jax.nn.silu(jnp.einsum('bsd,dh->bsh', x, W1[e]))
                val = jnp.einsum('bsd,dh->bsh', x, W3[e])
                y = jnp.einsum('bsh,hd->bsd', gate * val, W2[e])
                out = out + combine[..., e:e + 1] * y
            return out
        return _moe(x, Wg, W1, W3, W2)

    def _L3_xattn_ref(q, k, v):
        import jax, jax.numpy as jnp
        import numpy as np
        N_HEAD = 8
        b, d, m = q.shape
        c = v.shape[1]
        h = N_HEAD
        qh = q.reshape(b * h, d // h, m)
        kh = k.reshape(b * h, d // h, -1)
        vh = v.reshape(b * h, c // h, -1)
        scale = 1.0 / jnp.sqrt(jnp.asarray(d // h, dtype=q.dtype))
        qk = jnp.einsum('bdm,bdn->bmn', qh, kh) * scale
        sm = jax.nn.softmax(qk, axis=-1)
        ret = jnp.einsum('bmn,bcn->bcm', sm, vh)
        return ret.reshape(b, c, m)

    def _L3_ffn_ref(hidden_states, W_q, keys, down_embed, up_embed, gate_w, up_w, down_w):
        import jax, jax.numpy as jnp
        import numpy as np
        HIDDEN = 256
        INTER = 1024
        RETRIEVAL = 128
        NUM_EXPERTS = 512
        NUM_KEYS = 64
        TOP_K = 8
        B, S = (4, 256)
        b, s, h = hidden_states.shape
        n = b * s
        queries = (hidden_states @ W_q).reshape(2, n, RETRIEVAL // 2)
        routing = jnp.einsum('tnd,tdk->tnk', queries, keys)
        scores2, idx2 = jax.lax.top_k(routing, TOP_K)
        sx, sy = (scores2[0], scores2[1])
        ix, iy = (idx2[0], idx2[1])
        all_scores = (sx[:, :, None] + sy[:, None, :]).reshape(n, TOP_K * TOP_K)
        all_idx = (ix[:, :, None] * NUM_KEYS + iy[:, None, :]).reshape(n, TOP_K * TOP_K)
        scores, pk = jax.lax.top_k(all_scores, TOP_K)
        indices = jnp.take_along_axis(all_idx, pk, axis=-1)
        de = down_embed[indices]
        ue = up_embed[indices]
        x = hidden_states.reshape(n, h)
        ew = jnp.einsum('nh,nkh->nk', x, de)
        ew = jax.nn.silu(ew) * jax.nn.softmax(scores, axis=-1)
        experts_states = jnp.einsum('nk,nkh->nh', ew, ue).reshape(b, s, h)
        mlp = jax.nn.silu(x @ gate_w) * (x @ up_w) @ down_w
        return mlp.reshape(b, s, h) + experts_states
    x = x + _L0_xattn_ref(_layernorm(x, axis=-1), ctx_2048, L0_xattn_wq, L0_xattn_bq, L0_xattn_wkv, L0_xattn_bkv, L0_xattn_wp, L0_xattn_bp)
    x = x + _L0_ffn_ref(_layernorm(x, axis=-1), L0_ffn_gate_weight, L0_ffn_gate_w, L0_ffn_up_w, L0_ffn_down_w, L0_ffn_sh_gate_w, L0_ffn_sh_up_w, L0_ffn_sh_down_w)
    x = x + _L1_xattn_ref(_layernorm(x, axis=-1), ctx_2048, L1_xattn_Wq, L1_xattn_Wk, L1_xattn_Wv, L1_xattn_Wo)
    x = x + _L1_ffn_ref(_layernorm(x, axis=-1), L1_ffn_W, L1_ffn_b, L1_ffn_lora_A, L1_ffn_lora_B, L1_ffn_gate_w, L1_ffn_gate_b)
    x = x + _L2_xattn_ref(_layernorm(x, axis=-1), ctx_2048, ctx_2048, L2_xattn_Wh, L2_xattn_wg_w, L2_xattn_wo_w, L2_xattn_gn_gamma, L2_xattn_gn_beta)
    x = x + _L2_ffn_ref(_layernorm(x, axis=-1), L2_ffn_Wg, L2_ffn_W1, L2_ffn_W3, L2_ffn_W2)
    x = x + _L3_xattn_ref(_layernorm(x, axis=-1), ctx_2048, ctx_2048)
    x = x + _L3_ffn_ref(_layernorm(x, axis=-1), L3_ffn_W_q, L3_ffn_keys, L3_ffn_down_embed, L3_ffn_up_embed, L3_ffn_gate_w, L3_ffn_up_w, L3_ffn_down_w)
    return x

_drawn_inputs = setup_inputs


def setup_inputs(seed=0):
    import zlib

    import numpy as np

    out = dict(_drawn_inputs(seed))
    spreads = {'L2_xattn_gn_gamma': (1.0, 0.6), 'L2_xattn_gn_beta': (0.0, 1.483)}
    factors = {'L0_xattn_wq': 8.0,
     'L0_xattn_bq': 186.969,
     'L0_xattn_bkv': 5.035,
     'L0_ffn_gate_weight': 7.823,
     'L0_ffn_gate_w': 7.723,
     'L0_ffn_up_w': 8.0,
     'L0_ffn_down_w': 6.84,
     'L1_ffn_b': 37.33,
     'L1_ffn_gate_b': 32.536,
     'L3_ffn_W_q': 200.0,
     'L3_ffn_keys': 200.0,
     'L3_ffn_down_embed': 28.172,
     'L3_ffn_up_embed': 28.389,
     'L3_ffn_gate_w': 3.922,
     'L3_ffn_up_w': 3.899,
     'L3_ffn_down_w': 3.913,
     'L0_ffn_sh_gate_w': 8.0,
     'L0_ffn_sh_up_w': 8.0,
     'L0_ffn_sh_down_w': 8.0,
     'L1_ffn_lora_A': 4.449,
     'L1_ffn_lora_B': 4.663,
     'L1_ffn_gate_w': 5.186,
     'L1_xattn_Wq': 3.291,
     'L1_xattn_Wk': 3.42}
    for name, (base, spread) in spreads.items():
        noise = np.random.default_rng([zlib.crc32(name.encode()), seed]).standard_normal(out[name].shape)
        drawn = base * np.exp(spread * noise) if base else spread * noise
        out[name] = jnp.asarray(drawn.astype(out[name].dtype))
    for name, factor in factors.items():
        out[name] = (out[name] * factor).astype(out[name].dtype)
    return out
```

```python
from contextlib import ExitStack, contextmanager

import concourse.bass as bass
import numpy as np
from concourse import mybir

F32 = mybir.dt.float32
I32 = mybir.dt.int32
U32 = mybir.dt.uint32
ALU = mybir.AluOpType
ACT = mybir.ActivationFunctionType
AX = mybir.AxisListType

P = 128
T = 1024
D = 256
KB = D // P
NT = T // P
SEQ = 64
SEQS = T // SEQ
LOADED = 16
CREDIT = 2
ROUND = 12582912.0
LN_EPS = 1e-5
GN_EPS = 1e-3
EXPERTS = 8
SLOTS = 2 * T // P + EXPERTS - 1
PEER_KEYS = 64
PEER_TOP = 8
PEER_EXPERTS = 512
LAYERS = 8


class Chain:

    def __init__(self, eng, sem, passed):
        self.eng, self.sem, self.passed, self.base, self.n = eng, sem, passed, 0, 0

    def step(self, ins):
        ins.then_inc(self.sem, 1)
        self.n += 1
        self.eng.wait_ge(self.sem, self.base + self.n)

    def mark(self, ins):
        ins.then_inc(self.sem, 1)
        self.n += 1

    def wait(self):
        self.eng.wait_ge(self.sem, self.base + self.n)

    def step_fixed(self, ins):
        self.step(ins)
        self.apart()

    def apart(self):
        self.eng.sem_inc(self.passed, 1)

    @contextmanager
    def loop(self, trips, per):
        start = self.base + self.n
        with self.eng.Fori(0, trips) as i:
            self.base, self.n = i * per + start, 0
            yield i
            assert self.n == per, (self.n, per)
        self.base, self.n = start + trips * per, 0


class Core:

    def __init__(self, nc, ctx, dram):
        self.nc, self.ctx, self.dram = nc, ctx, dram
        self.masks_made = 0
        self.chains = {}

    def sb(self, name, shape, dt=F32):
        return self.ctx.enter_context(self.nc.sbuf_tensor(name, shape, dt))

    def sem(self, name):
        return self.ctx.enter_context(self.nc.semaphore(name))

    def count_masks(self, n):
        self.masks_made += n
        return self.masks_made - n

    def chain(self, eng, name):
        if name not in self.chains:
            self.chains[name] = Chain(eng, self.sem(name + "_own"), self.passed)
        return self.chains[name]


class Arena:

    def __init__(self, buf, width):
        self.buf, self.width, self.at = buf, width, 0

    def take(self, *dims, dt=F32, rows=P):
        n = int(np.prod(dims))
        assert self.at + n <= self.width, (self.at, n, self.width)
        ap = self.buf[0:rows, self.at:self.at + n]
        self.at += n
        if dt != F32:
            ap = ap.bitcast(dt)
        if len(dims) > 1:
            names = "abcde"[:len(dims)]
            ap = ap.rearrange(f"p ({' '.join(names)}) -> p {' '.join(names)}",
                              **{c: d for c, d in zip(names[1:], dims[1:])})
        return ap


def bc(ap, axis, n):
    shape = list(ap.shape)
    return ap.unsqueeze(axis).broadcast_to(shape[:axis] + [n] + shape[axis:])


def shared(nc, ctx, dram):
    k = Core(nc, ctx, dram)
    k.X = k.sb("X", [P, NT, D])
    k.CTXT = k.sb("CTXT", [P, KB, T])
    k.XNT = k.sb("XNT", [P, KB, T])
    k.xs = [k.sb(f"xs{p}", [P, D]) for p in (0, 1)]
    k.xT = [k.sb(f"xT{p}", [P, KB, P]) for p in (0, 1)]
    k.st = [k.sb(f"st{p}", [P, 6]) for p in (0, 1)]
    k.mv = [k.sb(f"mv{p}", [P, 2]) for p in (0, 1)]
    k.ve = [k.sb(f"ve{p}", [P, 1]) for p in (0, 1)]
    k.rstd = [k.sb(f"rstd{p}", [P, 1]) for p in (0, 1)]
    k.ident = k.sb("ident", [P, P])
    k.ones = k.sb("ones", [P, P])
    k.tri = k.sb("tri", [P, P])
    k.lower = k.sb("lower", [P, EXPERTS, EXPERTS])
    k.slot_no = k.sb("slot_no", [P, SLOTS])
    k.zeros = k.sb("zeros", [P, D])
    k.half = k.sb("half", [P, 1])
    k.bank = k.ctx.enter_context(nc.psum_tensor("bank", [P, 8, 512], F32))
    k.arena_buf = k.sb("arena", [P, 16200])
    k.early = k.sb("early", [P, 13200])
    k.late = k.sb("late", [P, 8800])
    k.x_tile = k.sem("x_tile")
    k.ctx_ld = k.sem("ctx_ld")
    k.const = k.sem("const")
    k.masks = k.sem("masks")
    k.passed = k.sem("passed")
    k.ln_var = k.sem("ln_var")
    k.ln_rstd = k.sem("ln_rstd")
    k.ln_out = k.sem("ln_out")
    k.xt_ps = k.sem("xt_ps")
    k.xt_sb = k.sem("xt_sb")
    k.z_ld = k.sem("z_ld")
    k.CONST = 12
    return k


def constants(k):
    def pool(e):
        e.memset(k.ident[:, :], 0.0).then_inc(k.const, 1)
        e.memset(k.ones[:, :], 1.0).then_inc(k.const, 1)
        e.memset(k.tri[:, :], 1.0).then_inc(k.const, 1)
        e.memset(k.lower[:, :, :], 1.0).then_inc(k.const, 1)
        e.memset(k.zeros[:, :], 0.0).then_inc(k.const, 1)
        e.memset(k.half[:, :], -0.5).then_inc(k.const, 1)
        e.iota(k.slot_no[:, :], pattern=[[1, SLOTS]], base=0, channel_multiplier=0,
               allow_small_or_imprecise_dtypes=True).then_inc(k.const, 1)
        e.wait_ge(k.const, 7)
        e.affine_select(out=k.ident[:, :], in_=k.ident[:, :], compare_op=ALU.not_equal, fill=1.0,
                        base=0, pattern=[[-1, P]], channel_multiplier=1).then_inc(k.const, 1)
        e.affine_select(out=k.tri[:, :], in_=k.tri[:, :], compare_op=ALU.is_ge, fill=0.0,
                        base=-1, pattern=[[1, P]], channel_multiplier=-1).then_inc(k.const, 1)
        e.affine_select(out=k.lower[:, :, :], in_=k.lower[:, :, :], compare_op=ALU.is_ge, fill=0.0,
                        base=-1, pattern=[[1, EXPERTS], [-1, EXPERTS]], channel_multiplier=0)\
            .then_inc(k.const, 1)
        e.wait_ge(k.const, 10)
        e.sem_inc(k.const, 2)
        e.wait_ge(k.ctx_ld, 16)

    def pe(e):
        e.sem_inc(k.xt_ps, CREDIT)
        e.wait_ge(k.const, k.CONST)
        e.wait_ge(k.ctx_ld, 16)

    def act(e):
        e.sem_inc(k.xt_sb, CREDIT)

    def dve(e):
        e.wait_ge(k.const, k.CONST)

    def sp(e):
        e.wait_ge(k.const, k.CONST)
        e.dma_start(k.dram["xg"].rearrange("(s p) d -> p s d", p=P), bc(k.zeros[:, :], 1, SLOTS))\
            .then_inc(k.z_ld, 16)

    return dict(sp=sp, pool=pool, pe=pe, act=act, dve=dve)


def ln_stats_dve(e, k, ch, t, p):
    ch.step_fixed(e.bn_stats(k.st[p][:, :], k.X[:, t, :]))
    ch.step(e.bn_aggr(k.mv[p][:, :], k.st[p][:, :]))
    e.tensor_scalar(k.ve[p][:, :], k.mv[p][:, 1:2], LN_EPS, None, ALU.add).then_inc(k.ln_var, 1)


def ln_rstd_pool(e, k, at, p):
    e.wait_ge(k.ln_var, at + 1)
    e.tensor_tensor(k.rstd[p][:, :], k.ve[p][:, :], k.half[:, :], ALU.pow).then_inc(k.ln_rstd, 1)


def ln_norm_dve(e, k, at, t, p):
    e.wait_ge(k.ln_rstd, at + 1)
    e.wait_ge(k.xt_ps, at + 1)
    return e.tensor_scalar(k.xs[p][:, :], k.X[:, t, :], k.mv[p][:, 0:1], k.rstd[p][:, 0:1],
                           ALU.subtract, ALU.mult)


def ln_pair_dve(e, k, ch, at0, i):
    for p in (0, 1):
        ln_stats_dve(e, k, ch, i * 2 + p, p)
    for p in (0, 1):
        ln_norm_dve(e, k, i * 2 + (at0 + p), i * 2 + p, p).then_inc(k.ln_out, 1)


def pairs_ahead(ch, per, normalise, body):
    with ch.loop(NT // 2 - 1, per) as i:
        body(i, lambda: normalise(i + 1))
    body(NT // 2 - 1, lambda: None)


def ln_tiles_dve(e, k, ch, at0, free=None, then=None):
    def stats(i):
        for p in (0, 1):
            ln_stats_dve(e, k, ch, i * 2 + p, p)

    def body(i, ahead):
        for p in (0, 1):
            if free:
                free(i, p)
            ln_norm_dve(e, k, i * 2 + (at0 + p), i * 2 + p, p).then_inc(k.ln_out, 1)
        ahead()
        if then:
            for p in (0, 1):
                then(i, p)

    stats(0)
    pairs_ahead(ch, 4, stats, body)


def ln_turn_pe(e, k, at, p, b):
    e.wait_ge(k.ln_out, at + 1)
    e.wait_ge(k.xt_sb, at + 1)
    for kb in range(KB):
        ins = e.transpose(k.bank[:, b, kb * P:(kb + 1) * P], k.xs[p][:, kb * P:(kb + 1) * P],
                          k.ident[:, :])
    ins.then_inc(k.xt_ps, 1)


def ln_copy_act(e, k, at, dst, b):
    e.wait_ge(k.xt_ps, at + 1 + CREDIT)
    e.copy(dst, k.bank[:, b, 0:D].rearrange("p (k m) -> p k m", k=KB)).then_inc(k.xt_sb, 1)


def qdq_dve(e, ch, src, dst, s3):
    am, s, rs = s3[:, 0:1], s3[:, 1:2], s3[:, 2:3]
    ch.step(e.tensor_reduce(am, src, AX.X, ALU.max, apply_absolute_value=True))
    ch.step(e.tensor_scalar(s, am, 1.0 / 127.0, 1e-8, ALU.mult, ALU.max))
    ch.step(e.reciprocal(rs, s))
    ch.step(e.tensor_scalar(dst, src, rs, 127.0, ALU.mult, ALU.min))
    ch.step(e.tensor_scalar(dst, dst, -127.0, ROUND, ALU.max, ALU.add))
    return e.tensor_scalar(dst, dst, ROUND, s, ALU.subtract, ALU.mult)


QDQ_STEPS = 5


def mm(e, out, pairs, start=True, stop=True):
    for n, (a, b) in enumerate(pairs):
        ins = e.matmul(out, a, b, start=start and n == 0, stop=stop and n == len(pairs) - 1)
    return ins



def attention_qdq(k, l):
    H, HD = 16, 16
    HB = P // HD
    at0 = 8 * l
    done0 = LOADED + 8 * l
    A = Arena(k.arena_buf, 16200)
    W = Arena(k.early, 13200)
    wn = [W.take(KB, D) for _ in range(2)]
    wT = [W.take(KB, D) for _ in range(2)]
    wk, wv = W.take(KB, D), W.take(KB, D)
    bv, bp = W.take(D), W.take(D)
    bqk = W.take(4)
    mask = A.take(HB, SEQ)
    kbd = [A.take(KB, 2, HB, SEQ) for _ in (0, 1)]
    qT = [A.take(KB, P) for _ in (0, 1)]
    kT = [A.take(KB, P) for _ in (0, 1)]
    cd = [A.take(KB, 2, 2, SEQ) for _ in (0, 1)]
    vbd = [A.take(2, H // 2, 2, HD) for _ in (0, 1)]
    pr = [A.take(H, SEQ) for _ in (0, 1)]
    pT = [A.take(H // 2, P) for _ in (0, 1)]
    oT = [A.take(KB, P) for _ in (0, 1)]
    mx = [A.take(H) for _ in (0, 1)]
    sm = [A.take(H) for _ in (0, 1)]
    ri = [A.take(H) for _ in (0, 1)]
    os = [A.take(D) for _ in (0, 1)]
    tmp = [A.take(D) for _ in (0, 1)]
    s3 = [A.take(3) for _ in range(4)]
    S = {n: k.sem("a0_" + n) for n in
         ("w_ld", "w_dq", "w_ps", "w_sb", "cd", "qk_ps", "v_ps", "q_sb", "k_sb", "v_sb", "kbd",
          "s_ps", "d_sb", "p_sb", "pt_ps", "pt_act", "pt_dve", "o_ps", "o_sb", "ot_ps", "ot_sb", "y_ps")}
    g = k.dram
    masks0 = k.count_masks(5)

    def sp(e):
        for dst, src in ((wn[0], g["wq"]), (wn[1], g["wp"]), (wk, g["wkT"]), (wv, g["wvT"]),
                         (bqk, g["bqk"]), (bv, g["bv"].partition_broadcast(P)),
                         (bp, g["bp"].partition_broadcast(P))):
            e.dma_start(dst, src).then_inc(S["w_ld"], 16)

    def pool(e):
        e.memset(mask, 1.0).then_inc(k.masks, 1)
        for p in (0, 1):
            e.memset(vbd[p], 0.0).then_inc(k.masks, 1)
        e.wait_ge(k.masks, masks0 + 3)
        e.affine_select(out=mask, in_=mask, compare_op=ALU.is_ge, fill=0.0, base=0,
                        pattern=[[-HD, HB], [0, SEQ]], channel_multiplier=1).then_inc(k.masks, 1)
        e.wait_ge(k.masks, masks0 + 4)
        e.affine_select(out=mask, in_=mask, compare_op=ALU.is_ge, fill=0.0, base=HD - 1,
                        pattern=[[HD, HB], [0, SEQ]], channel_multiplier=-1).then_inc(k.masks, 1)
        e.wait_ge(k.masks, masks0 + 5)
        with e.Fori(0, NT // 2) as i:
            for p in (0, 1):
                ln_rstd_pool(e, k, i * 2 + (at0 + p), p)
            for p in (0, 1):
                t = i * 2 + p
                e.wait_ge(S["v_ps"], i * 2 + (p + 1))
                for kb in range(KB):
                    ins = e.tensor_copy(
                        cd[p][:, kb], bc(k.CTXT[:, kb, bass.ds(t * P, P)]
                                         .rearrange("p (b m) -> p b m", b=2), 2, 2))
                ins.then_inc(S["cd"], 1)
            for p in (0, 1):
                e.wait_ge(S["k_sb"], i * 2 + (p + 1))
                for kb in range(KB):
                    for b in (0, 1):
                        ins = e.tensor_tensor(kbd[p][:, kb, b], bc(kT[p][:, kb, b * SEQ:(b + 1) * SEQ], 1, HB),
                                              mask, ALU.mult)
                ins.then_inc(S["kbd"], 1)

    def dve(e):
        ch = k.chain(e, "dve")

        def normalise(i):
            for p in (0, 1):
                ln_stats_dve(e, k, ch, i * 2 + p, p)
            for p in (0, 1):
                ch.step(ln_norm_dve(e, k, i * 2 + (at0 + p), i * 2 + p, p))
                qdq_dve(e, ch, k.xs[p][:, :], k.xs[p][:, :], s3[p]).then_inc(k.ln_out, 1)

        e.wait_ge(k.x_tile, done0)
        normalise(0)
        e.wait_ge(S["w_ld"], 16 * 7)
        for w in (0, 1):
            for ob in range(KB):
                qdq_dve(e, ch, wn[w][:, ob], wn[w][:, ob], s3[2 + ob]).then_inc(S["w_dq"], 1)

        def body(i, ahead):
            for p in (0, 1):
                e.wait_ge(S["v_ps"], i * 2 + (p + 1 + CREDIT))
                for half in (0, 1):
                    r = slice(64 * half, 64 * half + 64)
                    ins = e.tensor_tensor(
                        vbd[p][r, :, :, half, :],
                        k.bank[r, 4 * p, :].rearrange("p (b h o d) -> p b h o d", b=2, o=2, d=HD)[:, :, :, half],
                        bc(bv[r, :].rearrange("p (h o d) -> p h o d", o=2, d=HD)[:, :, half], 1, 2),
                        ALU.add)
                ins.then_inc(S["v_sb"], 1)
            for p in (0, 1):
                e.wait_ge(S["s_ps"], i * 2 + (p + 1))
                s = k.bank[:, 4 * p + 2:4 * p + 4, :].rearrange("p b (h m) -> p (b h) m", m=SEQ)
                ch.step(e.tensor_reduce(mx[p], s, AX.X, ALU.max))
                e.tensor_tensor(pr[p], s, bc(mx[p], 2, SEQ), ALU.subtract).then_inc(S["d_sb"], 1)
            for p in (0, 1):
                e.wait_ge(S["p_sb"], i * 2 + (p + 1))
                ch.step(e.tensor_reduce(sm[p], pr[p], AX.X, ALU.add))
                e.reciprocal(ri[p], sm[p])
            for p in (0, 1):
                e.wait_ge(S["pt_ps"], i * 2 + (p + 1))
                e.tensor_copy(pT[p][:, 4:8], k.bank[:, 4 * p + 3, :].rearrange("p (h m) -> p h m", m=P))\
                    .then_inc(S["pt_dve"], 1)
            ahead()
            for p in (0, 1):
                e.wait_ge(S["o_ps"], i * 2 + (p + 1))
                ch.step(e.tensor_tensor(os[p].rearrange("p (h d) -> p h d", d=HD),
                                        k.bank[:, 4 * p, 0:D].rearrange("p (h d) -> p h d", d=HD),
                                        bc(ri[p], 2, HD), ALU.mult))
                qdq_dve(e, ch, os[p], os[p], s3[p]).then_inc(S["o_sb"], 1)
            for p in (0, 1):
                t = i * 2 + p
                e.wait_ge(S["y_ps"], i * 2 + (p + 1))
                ch.step(e.tensor_tensor(tmp[p], k.bank[:, 4 * p, 0:D], bp, ALU.add))
                e.tensor_tensor(k.X[:, t, :], k.X[:, t, :], tmp[p], ALU.add).then_inc(k.x_tile, 1)

        pairs_ahead(ch, 2 * (2 + (1 + QDQ_STEPS) + 1 + 1 + (1 + QDQ_STEPS) + 1), normalise, body)

    def act(e):
        for w in (0, 1):
            e.wait_ge(S["w_ps"], w + 1)
            e.copy(wT[w], k.bank[:, w, :].rearrange("p (k m) -> p k m", k=KB)).then_inc(S["w_sb"], 1)
        with e.Fori(0, NT // 2) as i:
            for p in (0, 1):
                ln_copy_act(e, k, i * 2 + (at0 + p), k.xT[p][:, :, :], 4 * p)
            for p in (0, 1):
                e.wait_ge(S["qk_ps"], i * 2 + (p + 1))
                for dst, n, sem in ((kT[p], 2, "k_sb"), (qT[p], 0, "q_sb")):
                    for ob in range(KB):
                        ins = e.activation(dst[:, ob], k.bank[:, 4 * p + 1, (n + ob) * P:(n + ob + 1) * P],
                                           ACT.Identity, bias=bqk[:, n + ob:n + ob + 1])
                    ins.then_inc(S[sem], 1)
            for p in (0, 1):
                e.wait_ge(S["d_sb"], i * 2 + (p + 1))
                e.activation(pr[p], pr[p], ACT.Exp, scale=float(HD) ** -0.5).then_inc(S["p_sb"], 1)
            for p in (0, 1):
                e.wait_ge(S["pt_ps"], i * 2 + (p + 1))
                e.copy(pT[p][:, 0:4], k.bank[:, 4 * p + 2, :].rearrange("p (h m) -> p h m", m=P))\
                    .then_inc(S["pt_act"], 1)
            for p in (0, 1):
                e.wait_ge(S["ot_ps"], i * 2 + (p + 1))
                e.copy(oT[p], k.bank[:, 4 * p + 1, 0:D].rearrange("p (k m) -> p k m", k=KB))\
                    .then_inc(S["ot_sb"], 1)

    def pe(e):
        bank = k.bank
        e.sem_inc(S["v_ps"], CREDIT)
        for w in (0, 1):
            e.wait_ge(S["w_dq"], 2 * w + 2)
            for ob in range(KB):
                for kb in range(KB):
                    ins = e.transpose(bank[:, w, kb * D + ob * P:kb * D + (ob + 1) * P],
                                      wn[w][:, ob, kb * P:(kb + 1) * P], k.ident[:, :])
            ins.then_inc(S["w_ps"], 1)
        e.wait_ge(S["w_sb"], 2)
        with e.Fori(0, NT // 2) as i:
            for p in (0, 1):
                e.wait_ge(k.x_tile, i * 2 + (done0 + p - 1))
                ln_turn_pe(e, k, i * 2 + (at0 + p), p, 4 * p)
            for p in (0, 1):
                t = i * 2 + p
                e.wait_ge(k.xt_sb, i * 2 + (at0 + p + 1 + CREDIT))
                for ob in range(KB):
                    o = slice(ob * P, (ob + 1) * P)
                    mm(e, bank[:, 4 * p + 1, ob * P:(ob + 1) * P],
                       [(wT[0][:, kb, o], k.xT[p][:, kb, :]) for kb in range(KB)])
                    ins = mm(e, bank[:, 4 * p + 1, (2 + ob) * P:(3 + ob) * P],
                             [(wk[:, kb, o], k.CTXT[:, kb, bass.ds(t * P, P)]) for kb in range(KB)])
                ins.then_inc(S["qk_ps"], 1)
                e.wait_ge(S["cd"], i * 2 + (p + 1))
                for b in (0, 1):
                    ins = mm(e, bank[:, 4 * p, b * D:(b + 1) * D],
                             [(cd[p][:, kb, b].rearrange("p c m -> p (c m)"), wv[:, kb]) for kb in range(KB)])
                ins.then_inc(S["v_ps"], 1)
            for p in (0, 1):
                e.wait_ge(S["q_sb"], i * 2 + (p + 1))
                e.wait_ge(S["kbd"], i * 2 + (p + 1))
                for kb in range(KB):
                    for b in (0, 1):
                        r = slice(b * SEQ, (b + 1) * SEQ)
                        ins = e.matmul(bank[r, 4 * p + 2 + kb, :], qT[p][:, kb, r],
                                       kbd[p][:, kb, b].rearrange("p h m -> p (h m)"), start=True, stop=True)
                ins.then_inc(S["s_ps"], 1)
            for p in (0, 1):
                e.wait_ge(S["p_sb"], i * 2 + (p + 1))
                for h2 in range(H // 2):
                    ins = e.transpose(bank[:, 4 * p + 2 + h2 // 4, (h2 % 4) * P:(h2 % 4 + 1) * P],
                                      pr[p][:, 2 * h2:2 * h2 + 2].rearrange("p h m -> p (h m)"), k.ident[:, :])
                ins.then_inc(S["pt_ps"], 1)
            for p in (0, 1):
                e.wait_ge(S["pt_act"], i * 2 + (p + 1))
                e.wait_ge(S["pt_dve"], i * 2 + (p + 1))
                e.wait_ge(S["v_sb"], i * 2 + (p + 1))
                for h2 in range(H // 2):
                    for b in (0, 1):
                        r = slice(b * SEQ, (b + 1) * SEQ)
                        ins = e.matmul(bank[r, 4 * p, h2 * 2 * HD:(h2 + 1) * 2 * HD], pT[p][:, h2, r],
                                       vbd[p][:, b, h2].rearrange("p o d -> p (o d)"), start=True, stop=True)
                ins.then_inc(S["o_ps"], 1)
            for p in (0, 1):
                e.wait_ge(S["o_sb"], i * 2 + (p + 1))
                for kb in range(KB):
                    ins = e.transpose(bank[:, 4 * p + 1, kb * P:(kb + 1) * P], os[p][:, kb * P:(kb + 1) * P],
                                      k.ident[:, :])
                ins.then_inc(S["ot_ps"], 1)
            for p in (0, 1):
                e.wait_ge(S["ot_sb"], i * 2 + (p + 1))
                mm(e, bank[:, 4 * p, 0:D], [(oT[p][:, kb], wT[1][:, kb]) for kb in range(KB)])\
                    .then_inc(S["y_ps"], 1)

    return dict(sp=sp, pool=pool, dve=dve, act=act, pe=pe)



def rank_dve(e, ch, k, mask, s, n, ra, rb):
    groups = s.shape[1]
    a = ra.rearrange("p (g i j) -> p g i j", i=n, j=n)[:, 0:groups]
    b = rb.rearrange("p (g i j) -> p g i j", i=n, j=n)[:, 0:groups]
    ch.mark(e.tensor_tensor(a, bc(s, 2, n), bc(s, 3, n), ALU.is_gt))
    ch.step(e.tensor_tensor(b, bc(s, 2, n), bc(s, 3, n), ALU.is_equal))
    ch.step(e.tensor_tensor(b, b, bc(k.lower[:, 0:n, 0:n], 1, groups), ALU.mult))
    ch.step(e.tensor_tensor(a, a, b, ALU.add))
    ch.step(e.tensor_reduce(mask, a, AX.X, ALU.add))
    ch.step(e.tensor_scalar(mask, mask, 2.0, None, ALU.is_lt))


RANK_STEPS = 6


def experts(k, l, F, chunk, sizes, wbuf, shared_expert, prefix):
    E = EXPERTS
    NC = F // chunk
    NB = len(sizes)
    at0, done0 = 8 * l, LOADED + 8 * l
    DEEP = 3
    full = [n for n, s in enumerate(sizes) if s == sizes[0]]
    A = Arena(k.arena_buf, 16200)
    XN = A.take(NT, D)
    W = Arena(wbuf, wbuf.shape[1])
    gw = W.take(KB, E)
    if shared_expert:
        FS, SB = 352, (128, 128, 96)
        shg, shu, shd = W.take(KB, FS), W.take(KB, FS), W.take(len(SB), D)
        shT = [A.take(KB, P) for _ in (0, 1)]
        sh1 = [A.take(FS) for _ in (0, 1)]
        shhT = [A.take(len(SB), P) for _ in (0, 1)]
    wgu = [W.take(KB, 2 * F) for _ in range(DEEP)]
    wd = [W.take(NB, D) for _ in range(DEEP)]
    LG, EX, W8, MK, PRE, CN, OFF, DM = [A.take(NT, E) for _ in range(8)]
    RA, RB = A.take(NT * E * E), A.take(NT * E * E)
    mxr, smr, rir, dA, dB, sumd = [A.take(NT) for _ in range(6)]
    wA, wB = A.take(NT), A.take(NT)
    GS, GM = A.take(NT, 4), A.take(NT, 4)
    tot, cc, bx, bend = [A.take(E) for _ in range(4)]
    idx = A.take(2, NT, dt=I32)
    EQ = A.take(SLOTS, E)
    eidf = A.take(SLOTS)
    eid = A.take(SLOTS, dt=I32)
    xg = [A.take(D) for _ in range(DEEP)]
    xgT = [A.take(KB, P) for _ in range(DEEP)]
    h1, hh = A.take(F), A.take(F)
    hT = A.take(NB, P)
    ys = [A.take(D) for _ in range(DEEP)]
    ya = [A.take(D) for _ in range(4)]
    S = {n: k.sem(f"{prefix}_" + n) for n in
         ("w_ld", "w0", "w1", "w2", "xn", "lg_ps", "lg_sb", "routed", "scat", "gu_ps", "hs",
          "h_sb", "ht_ps", "ht_act", "ht_dve", "xg", "xgt_ps", "xgt_sb", "y_ps", "y_sb",
          "y_st0", "y_st1", "y_st2", "ga0", "ga1")}
    if shared_expert:
        for n in ("st", "st_free", "gu", "s1", "h", "tp", "tsb", "yps"):
            S["sh_" + n] = k.sem(f"{prefix}_sh_" + n)
    g = k.dram
    xg_d, yg_d = g["xg"], g["yg"]
    nld = 3 if len(full) == NB else 4
    MX, EX_, MK_, CNT_PS, IDX = range(1, 6)
    wsem = [S["w0"], S["w1"], S["w2"]]
    ysem = [S["y_st0"], S["y_st1"], S["y_st2"]]
    gsem = [S["ga0"], S["ga1"]]

    def slots(e, body):
        body(0, 0, 0, True, False)
        with e.Fori(0, (SLOTS - 2) // DEEP) as i:
            for q in range(1, DEEP + 1):
                body(i * DEEP + q, i + q // DEEP, q % DEEP, False, False)
        body(SLOTS - 1, (SLOTS - 1) // DEEP, (SLOTS - 1) % DEEP, False, True)

    def before(r, p):
        return (r, p - 1) if p > 0 else (r - 1, DEEP - 1)

    def after(r, p):
        return (r, p + 1) if p < DEEP - 1 else (r + 1, 0)

    def sp(e):
        if not shared_expert:
            e.wait_ge(k.x_tile, LOADED + 8 * min(l, 2))
        e.dma_start(gw, g[prefix + "_gate"]).then_inc(S["w_ld"], 16)
        if shared_expert:
            e.dma_start(shg, g["sh_g"]).then_inc(S["w_ld"], 16)
            e.dma_start(shu, g["sh_u"]).then_inc(S["w_ld"], 16)
            e.dma_start(shd[:, 0:2], g["sh_d"][0:256].rearrange("(b p) d -> p b d", p=P)).then_inc(S["w_ld"], 16)
            e.dma_start(shd[0:96, 2], g["sh_d"][256:352]).then_inc(S["w_ld"], 16)
        e.wait_ge(S["routed"], IDX)
        def body(s, r, p, first, last):
            if not first:
                e.wait_ge(S["y_ps"], s)
            v = e.value_load(eid[0:1, bass.ds(s, 1)] if not isinstance(s, int) else eid[0:1, s:s + 1],
                             min_val=0, max_val=E - 1)
            e.dma_start(wgu[p], g[prefix + "_gu"][bass.ds(v, 1)].rearrange("e p k f -> p (e k) f")).then_inc(wsem[p], 16)
            nf = len(full)
            e.dma_start(wd[p][0:sizes[0], 0:nf],
                        g[prefix + "_d"][bass.ds(v, 1), 0:nf * sizes[0]].rearrange("e (b p) d -> p (e b) d", p=sizes[0]))\
                .then_inc(wsem[p], 16)
            if nf < NB:
                e.dma_start(wd[p][0:sizes[-1], NB - 1],
                            g[prefix + "_d"][bass.ds(v, 1), nf * sizes[0]:F].rearrange("e p d -> p (e d)")).then_inc(wsem[p], 16)
            if first:
                e.wait_ge(S["scat"], 16 * 2 * NT)
            src = xg_d[s * P:(s + 1) * P, :] if isinstance(s, int) else xg_d[bass.ds(s * P, P), :]
            e.dma_start(xg[p], src).then_inc(wsem[p], 16)
        slots(e, body)

    def pool(e):
        e.sem_inc(S["xn"], CREDIT)
        with e.Fori(0, NT // 2) as i:
            for p in (0, 1):
                ln_rstd_pool(e, k, i * 2 + (at0 + p), p)
            for p in (0, 1):
                t = i * 2 + p
                e.wait_ge(k.ln_out, i * 2 + (at0 + p + 1))
                e.tensor_copy(XN[:, bass.ds(t, 1)].rearrange("p a d -> p (a d)"), k.xs[p][:, :]).then_inc(S["xn"], 1)
        e.wait_ge(S["xn"], NT + CREDIT)
        e.wait_ge(S["routed"], IDX)
        e.wait_ge(k.z_ld, 16)
        for t in range(NT):
            for q in (0, 1):
                e.indirect_dma_start(xg_d, bass.IndirectOffsetOnAxis(ap=idx[:, q, t:t + 1], axis=0),
                                     XN[:, t], None).then_inc(S["scat"], 16)
        for p in range(DEEP):
            e.wait_ge(ysem[p], 16 * (1 + (SLOTS + DEEP - 1 - p) // DEEP))
        for t in range(NT):
            p = t % 2
            if t >= 2:
                e.wait_ge(k.x_tile, done0 + t - 1)
            for q in (0, 1):
                e.indirect_dma_start(ya[2 * p + q], None, yg_d,
                                     bass.IndirectOffsetOnAxis(ap=idx[:, q, t:t + 1], axis=0)).then_inc(gsem[p], 16)

    def dve(e):
        ch = k.chain(e, "dve")
        e.sem_inc(S["lg_sb"], CREDIT)
        e.sem_inc(S["y_sb"], 1)
        if shared_expert:
            e.sem_inc(S["sh_st_free"], CREDIT)

        def free(i, p):
            e.wait_ge(S["xn"], i * 2 + (p + 1))

        def logits(i, p):
            t = i * 2 + p
            e.wait_ge(S["lg_ps"], i * 2 + (p + 1))
            e.tensor_copy(LG[:, bass.ds(t, 1)].rearrange("p a e -> p (a e)"), k.bank[:, 4 + p, 0:E])\
                    .then_inc(S["lg_sb"], 1)

        ln_tiles_dve(e, k, ch, at0, free, logits)
        e.wait_ge(S["lg_sb"], NT + CREDIT)
        ch.step(e.tensor_reduce(mxr, LG, AX.X, ALU.max))
        e.tensor_tensor(EX, LG, bc(mxr, 2, E), ALU.subtract).then_inc(S["routed"], 1)
        e.wait_ge(S["routed"], EX_)
        ch.step(e.tensor_reduce(smr, EX, AX.X, ALU.add))
        ch.step(e.reciprocal(rir, smr))
        ch.step(e.tensor_tensor(EX, EX, bc(rir, 2, E), ALU.mult))
        if shared_expert:
            ch.step(e.tensor_reduce(GS, EX.rearrange("p t (g e) -> p t g e", g=4), AX.X, ALU.max))
            rank_dve(e, ch, k, GM, GS, 4, RA, RB)
            ch.step(e.tensor_tensor(EX.rearrange("p t (g e) -> p t g e", g=4),
                                    EX.rearrange("p t (g e) -> p t g e", g=4), bc(GM, 3, 2), ALU.mult))
        rank_dve(e, ch, k, MK, EX, E, RA, RB)
        e.tensor_tensor(W8, EX, MK, ALU.mult).then_inc(S["routed"], 1)
        e.wait_ge(S["routed"], MK_)
        if not shared_expert:
            ch.step(e.tensor_reduce(smr, W8, AX.X, ALU.add))
            ch.step(e.reciprocal(rir, smr))
            ch.step(e.tensor_tensor(W8, W8, bc(rir, 2, E), ALU.mult))
        e.wait_ge(S["routed"], CNT_PS)
        ch.mark(e.tensor_copy(PRE, k.bank[:, 6, 0:NT * E].rearrange("p (t e) -> p t e", e=E)))
        ch.mark(e.tensor_copy(CN, k.bank[:, 6, NT * E:2 * NT * E].rearrange("p (t e) -> p t e", e=E)))
        ch.step(e.memset(OFF[:, 0], 0.0))
        for t in range(1, NT):
            ch.step(e.tensor_tensor(OFF[:, t], OFF[:, t - 1], CN[:, t - 1], ALU.add))
        ch.step(e.tensor_tensor(tot, OFF[:, NT - 1], CN[:, NT - 1], ALU.add))
        ch.step(e.tensor_scalar(cc, tot, 1.0 / P, (P - 1.0) / P - 0.5 + 0.5 / P, ALU.mult, ALU.add))
        ch.step(e.tensor_scalar(cc, cc, ROUND, ROUND, ALU.add, ALU.subtract))
        ch.step(e.memset(bx[:, 0:1], 0.0))
        for x in range(1, E):
            ch.step(e.tensor_tensor(bx[:, x:x + 1], bx[:, x - 1:x], cc[:, x - 1:x], ALU.add))
        ch.mark(e.tensor_tensor(bend, bx, cc, ALU.add))
        ch.mark(e.tensor_tensor(PRE, PRE, OFF, ALU.add))
        ch.step(e.tensor_scalar(bx, bx, float(P), 1.0, ALU.mult, ALU.add))
        ch.step(e.tensor_tensor(PRE, PRE, bc(bx, 1, NT), ALU.add))
        ch.step(e.tensor_tensor(DM, PRE, MK, ALU.mult))
        ch.mark(e.tensor_reduce(dA, DM, AX.X, ALU.max))
        ch.step(e.tensor_reduce(sumd, DM, AX.X, ALU.add))
        ch.step(e.tensor_tensor(dB, sumd, dA, ALU.subtract))
        ch.mark(e.tensor_scalar(idx[:, 0], dA, -1.0, None, ALU.add))
        ch.mark(e.tensor_scalar(idx[:, 1], dB, -1.0, None, ALU.add))
        ch.step(e.tensor_tensor(EQ, bc(bend, 1, SLOTS), bc(k.slot_no[:, :], 2, E), ALU.is_le))
        ch.step(e.tensor_reduce(eidf, EQ, AX.X, ALU.add))
        e.tensor_scalar(eid, eidf, E - 1.0, None, ALU.min).then_inc(S["routed"], 1)
        for d, w in ((dA, wA), (dB, wB)):
            ch.step(e.tensor_tensor(CN, DM, bc(d, 2, E), ALU.is_equal))
            ch.step(e.tensor_tensor(CN, CN, W8, ALU.mult))
            ch.step(e.tensor_reduce(w, CN, AX.X, ALU.add))
        if shared_expert:
            with e.Fori(0, NT // 2) as i:
                for p in (0, 1):
                    e.wait_ge(S["sh_s1"], i * 2 + (p + 1))
                    e.tensor_tensor(sh1[p], sh1[p], k.bank[:, 4 * p + 1, 0:FS], ALU.mult).then_inc(S["sh_h"], 1)
                for p in (0, 1):
                    t = i * 2 + p
                    e.wait_ge(S["sh_yps"], i * 2 + (p + 1))
                    ins = e.tensor_tensor(k.X[:, t, :], k.X[:, t, :], k.bank[:, 4 * p + 3, 0:D], ALU.add)
                    ins.then_inc(S["sh_st_free"], 1)
            e.wait_ge(S["sh_st_free"], NT + CREDIT)

        def body(s, r, p, first, last):
            e.wait_ge(S["hs"], s + 1)
            e.tensor_tensor(hh.rearrange("p (n c) -> p n c", n=NC), h1.rearrange("p (n c) -> p n c", n=NC),
                            k.bank[:, NC:2 * NC, 0:chunk], ALU.mult).then_inc(S["h_sb"], 1)
            if not first:
                y_copy(s - 1, *before(r, p))
            if NB > 4:
                e.wait_ge(S["ht_ps"], s + 1)
                e.tensor_copy(hT[:, 4:NB - 1], k.bank[:, 5, 0:(NB - 5) * P].rearrange("p (b m) -> p b m", m=P))
                e.tensor_copy(hT[0:sizes[-1], NB - 1], k.bank[0:sizes[-1], 5, (NB - 5) * P:(NB - 4) * P])\
                    .then_inc(S["ht_dve"], 1)
            if last:
                y_copy(s, r, p)

        def y_copy(s, r, p):
            e.wait_ge(S["y_ps"], s + 1 + CREDIT)
            e.wait_ge(ysem[p], r * 16 + 16)
            e.tensor_copy(ys[p], k.bank[:, 6, 0:D]).then_inc(S["y_sb"], 1)
        slots(e, body)
        for t in range(NT):
            p = t % 2
            e.wait_ge(gsem[p], 32 * (t // 2 + 1))
            ch.step(e.scalar_tensor_tensor(k.X[:, t], ya[2 * p], wA[:, t:t + 1], k.X[:, t], ALU.mult, ALU.add))
            e.scalar_tensor_tensor(k.X[:, t], ya[2 * p + 1], wB[:, t:t + 1], k.X[:, t], ALU.mult, ALU.add)\
                .then_inc(k.x_tile, 1)

    def act(e):
        with e.Fori(0, NT // 2) as i:
            for p in (0, 1):
                t = i * 2 + p
                ln_copy_act(e, k, i * 2 + (at0 + p), k.xT[p][:, :, :], p)
                if shared_expert:
                    e.wait_ge(k.xt_sb, i * 2 + (at0 + p + 1 + CREDIT))
                    e.copy(k.XNT[:, :, bass.ds(t * P, P)], k.xT[p][:, :, :]).then_inc(S["sh_st"], 1)
        e.wait_ge(S["routed"], MX)
        e.activation(EX, EX, ACT.Exp).then_inc(S["routed"], 1)
        if shared_expert:
            e.wait_ge(S["sh_st"], NT)
            with e.Fori(0, NT // 2) as i:
                for p in (0, 1):
                    t = i * 2 + p
                    e.wait_ge(S["sh_st_free"], i * 2 + (p + 1))
                    e.copy(shT[p], k.XNT[:, :, bass.ds(t * P, P)]).then_inc(S["sh_st"], 1)
                for p in (0, 1):
                    e.wait_ge(S["sh_gu"], i * 2 + (p + 1))
                    e.activation(sh1[p], k.bank[:, 4 * p, 0:FS], ACT.Silu).then_inc(S["sh_s1"], 1)
                for p in (0, 1):
                    e.wait_ge(S["sh_tp"], i * 2 + (p + 1))
                    e.copy(shhT[p][:, 0:2], k.bank[:, 4 * p + 2, 0:2 * P].rearrange("p (b m) -> p b m", m=P))
                    e.copy(shhT[p][0:96, 2], k.bank[0:96, 4 * p + 2, 2 * P:3 * P]).then_inc(S["sh_tsb"], 1)

        def xg_copy(s, p):
            e.wait_ge(S["xgt_ps"], s + 1)
            e.copy(xgT[p], k.bank[:, 7, 0:D].rearrange("p (k m) -> p k m", k=KB)).then_inc(S["xgt_sb"], 1)

        def store(s, p):
            e.wait_ge(S["y_sb"], s + 2)
            dst = yg_d[s * P:(s + 1) * P, :] if isinstance(s, int) else yg_d[bass.ds(s * P, P), :]
            e.dma_start(dst, ys[p]).then_inc(ysem[p], 16)

        for p in range(DEEP):
            e.sem_inc(ysem[p], 16)

        def body(s, r, p, first, last):
            if first:
                xg_copy(0, 0)
            e.wait_ge(S["gu_ps"], s + 1)
            e.activation(h1.rearrange("p (n c) -> p n c", n=NC), k.bank[:, 0:NC, 0:chunk], ACT.Silu)\
                .then_inc(S["hs"], 1)
            if not last:
                xg_copy(s + 1, (p + 1) % DEEP)
            e.wait_ge(S["ht_ps"], s + 1)
            n = min(NB, 4)
            e.copy(hT[0:sizes[0], 0:n], k.bank[0:sizes[0], 4, 0:n * P].rearrange("p (b m) -> p b m", m=P))\
                .then_inc(S["ht_act"], 1)
            if not first:
                store(s - 1, (p - 1) % DEEP)
            if last:
                store(s, p)
        slots(e, body)

    def pe(e):
        bank = k.bank
        e.sem_inc(S["y_ps"], CREDIT)
        if shared_expert:
            e.wait_ge(S["w_ld"], 16 * 5)
        else:
            e.wait_ge(S["w_ld"], 16)
        with e.Fori(0, NT // 2) as i:
            for p in (0, 1):
                ln_turn_pe(e, k, i * 2 + (at0 + p), p, p)
            for p in (0, 1):
                e.wait_ge(k.xt_sb, i * 2 + (at0 + p + 1 + CREDIT))
                e.wait_ge(S["lg_sb"], i * 2 + (p + 1))
                mm(e, bank[:, 4 + p, 0:E], [(k.xT[p][:, kb, :], gw[:, kb]) for kb in range(KB)])\
                    .then_inc(S["lg_ps"], 1)
        e.wait_ge(S["routed"], MK_)
        m = MK.rearrange("p t e -> p (t e)")
        e.matmul(bank[:, 6, 0:NT * E], k.tri[:, :], m, start=True, stop=True)
        e.matmul(bank[:, 6, NT * E:2 * NT * E], k.ones[:, :], m, start=True, stop=True).then_inc(S["routed"], 1)
        if shared_expert:
            e.wait_ge(S["routed"], IDX)
            with e.Fori(0, NT // 2) as i:
                for p in (0, 1):
                    e.wait_ge(S["sh_st"], i * 2 + (NT + p + 1))
                    for w, b in ((shg, 4 * p), (shu, 4 * p + 1)):
                        ins = mm(e, bank[:, b, 0:FS], [(shT[p][:, kb], w[:, kb]) for kb in range(KB)])
                    ins.then_inc(S["sh_gu"], 1)
                for p in (0, 1):
                    e.wait_ge(S["sh_h"], i * 2 + (p + 1))
                    for b, n in enumerate(SB):
                        ins = e.transpose(bank[0:n, 4 * p + 2, b * P:(b + 1) * P], sh1[p][:, b * P:b * P + n],
                                          k.ident[:, :])
                    ins.then_inc(S["sh_tp"], 1)
                for p in (0, 1):
                    e.wait_ge(S["sh_tsb"], i * 2 + (p + 1))
                    mm(e, bank[:, 4 * p + 3, 0:D], [(shhT[p][0:n, b], shd[0:n, b]) for b, n in enumerate(SB)])\
                        .then_inc(S["sh_yps"], 1)
            e.wait_ge(S["sh_st_free"], NT + CREDIT)

        def xg_turn(s, r, p):
            e.wait_ge(wsem[p], r * (16 * nld) + 16 * nld)
            for kb in range(KB):
                ins = e.transpose(bank[:, 7, kb * P:(kb + 1) * P], xg[p][:, kb * P:(kb + 1) * P], k.ident[:, :])
            ins.then_inc(S["xgt_ps"], 1)

        def down(s, p):
            e.wait_ge(S["ht_act"], s + 1)
            if NB > 4:
                e.wait_ge(S["ht_dve"], s + 1)
            e.wait_ge(S["y_sb"], s + 1)
            mm(e, bank[:, 6, 0:D], [(hT[0:n, b], wd[p][0:n, b]) for b, n in enumerate(sizes)])\
                .then_inc(S["y_ps"], 1)

        def body(s, r, p, first, last):
            if first:
                xg_turn(0, 0, 0)
            e.wait_ge(S["xgt_sb"], s + 1)
            for c in range(2 * NC):
                ins = mm(e, bank[:, c, 0:chunk], [(xgT[p][:, kb], wgu[p][:, kb, c * chunk:(c + 1) * chunk])
                                                  for kb in range(KB)])
            ins.then_inc(S["gu_ps"], 1)
            if not first:
                down(s - 1, (p - 1) % DEEP)
            if not last:
                xg_turn(s + 1, *after(r, p))
            e.wait_ge(S["h_sb"], s + 1)
            for b, n in enumerate(sizes):
                ins = e.transpose(bank[0:n, 4 + b // 4, (b % 4) * P:(b % 4 + 1) * P],
                                  hh[:, sum(sizes[:b]):sum(sizes[:b]) + n], k.ident[:, :])
            ins.then_inc(S["ht_ps"], 1)
            if last:
                down(s, p)

        slots(e, body)

    return dict(sp=sp, pool=pool, dve=dve, act=act, pe=pe)



def attention_wide(k, l):
    H, HD = 16, 128
    HALF = T // 2
    at0, done0 = 8 * l, LOADED + 8 * l
    A = Arena(k.arena_buf, 16200)
    W = Arena(k.late, 8800)
    w3 = [W.take(3, KB, HD) for _ in (0, 1)]
    wo = [W.take(D) for _ in (0, 1)]
    qT = [A.take(T) for _ in (0, 1)]
    kT = [A.take(T) for _ in (0, 1)]
    v = [A.take(NT, HD) for _ in (0, 1)]
    s_sb = A.take(NT, SEQ)
    pb = A.take(NT, 2, SEQ)
    pT = A.take(NT, P)
    cT = A.take(T)
    mx, sm, ri = A.take(NT), A.take(NT), A.take(NT)
    S = {n: k.sem("a2_" + n) for n in
         ("w0", "w1", "o0", "o1", "s_ps", "d_sb", "p_sb", "pb", "qk_ps", "qk_sb", "v_ps", "v_sb", "pt_ps",
          "pt_act", "pt_dve", "wo_ps", "wo_sb", "c_ps", "c_sb")}
    wsem, osem = [S["w0"], S["w1"]], [S["o0"], S["o1"]]
    g = k.dram
    masks0 = k.count_masks(1)
    QK0, VB, TB, CB, SB_ = 0, 2, 2, 4, 6

    def heads(e, body):
        with e.Fori(0, H // 2) as i:
            for p in (0, 1):
                body(i * 2 + p, i, p)

    def sp(e):
        def load(h, p):
            row = bass.ds(h, 1)
            e.dma_start(w3[p], g["a2_qkv"][row].rearrange("h p c k f -> p (h c) k f")).then_inc(wsem[p], 16)

        def load_o(h, p):
            e.dma_start(wo[p], g["a2_o"][bass.ds(h, 1)].rearrange("h p d -> p (h d)")).then_inc(osem[p], 16)

        for p in (0, 1):
            load(p, p)
            load_o(p, p)
        with e.Fori(0, H // 2 - 1) as i:
            for p in (0, 1):
                e.wait_ge(S["v_ps"], i * 2 + (p + 1))
                load(i * 2 + (p + 2), p)
            for p in (0, 1):
                e.wait_ge(S["wo_ps"], (i * 2 + (p + 1)) * 4)
                load_o(i * 2 + (p + 2), p)

    def pool(e):
        e.memset(pb, 0.0).then_inc(k.masks, 1)
        with e.Fori(0, NT // 2) as i:
            for p in (0, 1):
                ln_rstd_pool(e, k, i * 2 + (at0 + p), p)

    def dve(e):
        ch = k.chain(e, "dve")
        e.sem_inc(S["wo_sb"], 2)
        ln_tiles_dve(e, k, ch, at0)
        e.wait_ge(k.masks, masks0 + 1)

        def v_copy(h, p):
            e.wait_ge(S["v_ps"], h + 1)
            e.tensor_copy(v[p], k.bank[:, VB:VB + 2, :].rearrange("p b (t d) -> p (b t) d", d=HD))\
                .then_inc(S["v_sb"], 1)

        def softmax(h, p):
            e.wait_ge(S["s_ps"], h + 1)
            s = k.bank[:, SB_, :].rearrange("p (t m) -> p t m", m=SEQ)
            ch.step(e.tensor_reduce(mx, s, AX.X, ALU.max))
            e.tensor_tensor(s_sb, s, bc(mx, 2, SEQ), ALU.subtract).then_inc(S["d_sb"], 1)
            e.wait_ge(S["p_sb"], h + 1)
            ch.step(e.tensor_reduce(sm, s_sb, AX.X, ALU.add))
            ch.step(e.reciprocal(ri, sm))
            e.tensor_tensor(pb[0:64, :, 0], s_sb[0:64], bc(ri[0:64], 2, SEQ), ALU.mult)
            e.tensor_tensor(pb[64:128, :, 1], s_sb[64:128], bc(ri[64:128], 2, SEQ), ALU.mult).then_inc(S["pb"], 1)

        def out_add(h):
            for j in range(4):
                e.wait_ge(S["wo_ps"], h * 4 + (j + 1))
                x = k.X[:, 2 * j:2 * j + 2].rearrange("p t d -> p (t d)")
                e.tensor_tensor(x, x, k.bank[:, QK0 + j % 2, :], ALU.add).then_inc(S["wo_sb"], 1)

        def pT_copy(h):
            e.wait_ge(S["pt_ps"], h + 1)
            e.tensor_copy(pT[:, 4:8], k.bank[:, TB + 1, :].rearrange("p (t m) -> p t m", m=P))\
                .then_inc(S["pt_dve"], 1)

        v_copy(0, 0)
        softmax(0, 0)
        v_copy(1, 1)
        pT_copy(0)
        with ch.loop(H // 2 - 1, 2 * 3) as i:
            for q in (1, 2):
                h, p = i * 2 + q, q % 2
                softmax(h, p)
                v_copy(h + 1, 1 - p)
                pT_copy(h)
                e.wait_ge(S["wo_sb"], i * 8 + (4 * (q - 1) + 2))
                out_add(h - 1)
        softmax(H - 1, 1)
        pT_copy(H - 1)
        e.wait_ge(S["wo_sb"], 4 * (H - 2) + 2)
        out_add(H - 2)
        e.wait_ge(S["wo_sb"], 4 * (H - 1) + 2)
        for j in range(4):
            e.wait_ge(S["wo_ps"], (H - 1) * 4 + (j + 1))
            for t in (2 * j, 2 * j + 1):
                e.tensor_tensor(k.X[:, t], k.X[:, t], k.bank[:, QK0 + j % 2, (t % 2) * D:(t % 2 + 1) * D],
                                ALU.add).then_inc(k.x_tile, 1)

    def act(e):
        with e.Fori(0, NT // 2) as i:
            for p in (0, 1):
                t = i * 2 + p
                ln_copy_act(e, k, i * 2 + (at0 + p), k.XNT[:, :, bass.ds(t * P, P)], p)

        def qk_copy(h, p):
            for n in range(4):
                e.wait_ge(S["qk_ps"], h * 4 + (n + 1))
                if n < 2:
                    ins = e.mul(qT[p][:, n * HALF:(n + 1) * HALF], k.bank[:, QK0 + n % 2, :], float(HD) ** -0.5)
                else:
                    ins = e.copy(kT[p][:, (n - 2) * HALF:(n - 1) * HALF], k.bank[:, QK0 + n % 2, :])
                ins.then_inc(S["qk_sb"], 1)

        def exp(h):
            e.wait_ge(S["d_sb"], h + 1)
            e.activation(s_sb, s_sb, ACT.Exp).then_inc(S["p_sb"], 1)

        def rest(h, p):
            e.wait_ge(S["pt_ps"], h + 1)
            e.copy(pT[:, 0:4], k.bank[:, TB, :].rearrange("p (t m) -> p t m", m=P)).then_inc(S["pt_act"], 1)
            e.wait_ge(S["c_ps"], h + 1)
            e.copy(cT, k.bank[:, CB:CB + 2, :].rearrange("p b n -> p (b n)")).then_inc(S["c_sb"], 1)

        e.sem_inc(S["qk_sb"], 2)
        qk_copy(0, 0)
        with e.Fori(0, H // 2 - 1) as i:
            for p in (0, 1):
                h = i * 2 + p
                exp(h)
                qk_copy(h + 1, 1 - p)
                rest(h, p)
        exp(H - 2)
        qk_copy(H - 1, 1)
        rest(H - 2, 0)
        exp(H - 1)
        rest(H - 1, 1)

    def pe(e):
        bank = k.bank
        with e.Fori(0, NT // 2) as i:
            for p in (0, 1):
                ln_turn_pe(e, k, i * 2 + (at0 + p), p, p)
        e.wait_ge(k.xt_sb, at0 + NT + CREDIT)

        def project(h, p, half):
            e.wait_ge(wsem[p], half * 16 + 16)
            for n in range(4):
                e.wait_ge(S["qk_sb"], h * 4 + (n + 1))
                src = k.XNT if n < 2 else k.CTXT
                mm(e, bank[:, QK0 + n % 2, :],
                   [(w3[p][:, n // 2, kb], src[:, kb, (n % 2) * HALF:(n % 2 + 1) * HALF]) for kb in range(KB)])\
                    .then_inc(S["qk_ps"], 1)
            for t in range(NT):
                ins = mm(e, bank[:, VB + t // 4, (t % 4) * HD:(t % 4 + 1) * HD],
                         [(k.CTXT[:, kb, t * P:(t + 1) * P], w3[p][:, 2, kb]) for kb in range(KB)])
            ins.then_inc(S["v_ps"], 1)

        def scores(h, p):
            e.wait_ge(S["qk_sb"], h * 4 + (4 + 2))
            for t in range(NT):
                for b in (0, 1):
                    c = slice((2 * t + b) * SEQ, (2 * t + b + 1) * SEQ)
                    ins = e.matmul(bank[b * SEQ:(b + 1) * SEQ, SB_, t * SEQ:(t + 1) * SEQ], qT[p][:, c], kT[p][:, c],
                                   start=True, stop=True)
            ins.then_inc(S["s_ps"], 1)

        def turn_p(h):
            e.wait_ge(S["pb"], h + 1)
            for t in range(NT):
                ins = e.transpose(bank[:, TB + t // 4, (t % 4) * P:(t % 4 + 1) * P],
                                  pb[:, t].rearrange("p b m -> p (b m)"), k.ident[:, :])
            ins.then_inc(S["pt_ps"], 1)

        def out_proj(h, p, half, last=False):
            e.wait_ge(osem[p], half * 16 + 16)
            e.wait_ge(S["c_sb"], h + 1)
            for j in range(4):
                if last and j >= 2:
                    e.wait_ge(k.x_tile, done0 + 2 * (j - 1))
                else:
                    e.wait_ge(S["wo_sb"], h * 4 + (j + 1))
                for q in (0, 1):
                    t = 2 * j + q
                    ins = e.matmul(bank[:, QK0 + j % 2, q * D:(q + 1) * D], cT[:, t * P:(t + 1) * P], wo[p],
                                   start=True, stop=True)
                ins.then_inc(S["wo_ps"], 1)

        def pv(h, p):
            e.wait_ge(S["pt_act"], h + 1)
            e.wait_ge(S["pt_dve"], h + 1)
            for t in range(NT):
                ins = e.matmul(bank[:, CB + t // 4, (t % 4) * P:(t % 4 + 1) * P], v[p][:, t], pT[:, t],
                               start=True, stop=True)
            ins.then_inc(S["c_ps"], 1)

        def head(h, p, half, first=False, last=False):
            scores(h, p)
            if not last:
                if not first:
                    e.wait_ge(S["wo_sb"], h * 4 + (2 - 4))
                project(h + 1, 1 - p, half)
                e.wait_ge(S["v_sb"], h + 2)
            turn_p(h)
            if not first:
                e.wait_ge(S["qk_sb"], h * 4 + (8 + 2 if not last else 4 + 2))
                out_proj(h - 1, 1 - p, half - 1 if not last else half)
            pv(h, p)

        project(0, 0, 0)
        head(0, 0, 0, first=True)
        with e.Fori(0, H // 2 - 1) as i:
            for q in (1, 2):
                head(i * 2 + q, q % 2, i + 1)
        head(H - 1, 1, (H - 2) // 2, last=True)
        out_proj(H - 1, 1, (H - 1) // 2, last=True)

    return dict(sp=sp, pool=pool, dve=dve, act=act, pe=pe)


class Stages:

    def __init__(self, sem, *names):
        self.sem, self.names = sem, names

    def at(self, i, p, name):
        return i * (2 * len(self.names)) + (2 * self.names.index(name) + p + 1)

    def done(self, ins):
        ins.then_inc(self.sem, 1)

    def wait(self, e, i, p, name):
        e.wait_ge(self.sem, self.at(i, p, name))


def tiles(e):
    return e.Fori(0, NT // 2)



def lora_mixture(k, l):
    E, R = EXPERTS, 16
    at0, done0 = 8 * l, LOADED + 8 * l
    A = Arena(k.arena_buf, 16200)
    W = Arena(k.late[:, 2100:4100], 2000)
    ga = W.take(KB, E + E * R)
    wt = W.take(KB, D)
    lb = W.take(D)
    bias, gb = W.take(D), W.take(E)
    lg = [A.take(1, E) for _ in (0, 1)]
    ex = [A.take(1, E) for _ in (0, 1)]
    mk = [A.take(1, E) for _ in (0, 1)]
    m1 = [A.take(1) for _ in (0, 1)]
    ra, rb = A.take(E * E), A.take(E * E)
    xa = [A.take(E, R) for _ in (0, 1)]
    xaT = [A.take(P) for _ in (0, 1)]
    tmp = [A.take(D) for _ in (0, 1)]
    ld = k.sem("l3_ld")
    pe_ = Stages(k.sem("l3_pe"), "xa", "turn", "y")
    dve_ = Stages(k.sem("l3_dve"), "shift", "xa")
    act_ = Stages(k.sem("l3_act"), "exp", "xaT")
    g = k.dram

    def sp(e):
        for dst, src in ((ga, g["l3_ga"]), (wt, g["l3_w"]), (lb, g["l3_b"]),
                         (bias, g["l3_bias"].partition_broadcast(P)), (gb, g["l3_gb"].partition_broadcast(P))):
            e.dma_start(dst, src).then_inc(ld, 16)

    def pool(e):
        with tiles(e) as i:
            for p in (0, 1):
                ln_rstd_pool(e, k, i * 2 + (at0 + p), p)

    def dve(e):
        ch = k.chain(e, "dve")
        e.wait_ge(ld, 16 * 5)

        def body(i, ahead):
            for p in (0, 1):
                pe_.wait(e, i, p, "xa")
                ch.step(e.tensor_tensor(lg[p][:, 0], k.bank[:, 4 * p + 1, 0:E], gb, ALU.add))
                ch.step(e.tensor_reduce(m1[p], lg[p], AX.X, ALU.max))
                dve_.done(e.tensor_scalar(ex[p][:, 0], lg[p][:, 0], m1[p], None, ALU.subtract))
                rank_dve(e, ch, k, mk[p], lg[p], E, ra, rb)
            for p in (0, 1):
                act_.wait(e, i, p, "exp")
                ch.step(e.tensor_tensor(ex[p], ex[p], mk[p], ALU.mult))
                ch.step(e.tensor_reduce(m1[p], ex[p], AX.X, ALU.add))
                ch.step(e.reciprocal(m1[p], m1[p]))
                ch.step(e.tensor_scalar(ex[p][:, 0], ex[p][:, 0], m1[p], None, ALU.mult))
                dve_.done(e.tensor_tensor(xa[p], k.bank[:, 4 * p + 1, E:E + E * R].rearrange("p (e r) -> p e r", r=R),
                                          bc(ex[p][:, 0], 2, R), ALU.mult))
            ahead()
            for p in (0, 1):
                t = i * 2 + p
                pe_.wait(e, i, p, "y")
                ch.step(e.tensor_tensor(tmp[p], k.bank[:, 4 * p + 2, 0:D], bias, ALU.add))
                e.tensor_tensor(k.X[:, t, :], k.X[:, t, :], tmp[p], ALU.add).then_inc(k.x_tile, 1)

        ln_pair_dve(e, k, ch, at0, 0)
        pairs_ahead(ch, 2 * (2 + 2 + RANK_STEPS + 4 + 1), lambda i: ln_pair_dve(e, k, ch, at0, i), body)

    def act(e):
        with tiles(e) as i:
            for p in (0, 1):
                ln_copy_act(e, k, i * 2 + (at0 + p), k.xT[p][:, :, :], 4 * p)
            for p in (0, 1):
                dve_.wait(e, i, p, "shift")
                act_.done(e.activation(ex[p], ex[p], ACT.Exp))
            for p in (0, 1):
                pe_.wait(e, i, p, "turn")
                act_.done(e.copy(xaT[p], k.bank[:, 4 * p + 3, 0:P]))

    def pe(e):
        bank = k.bank
        e.wait_ge(ld, 16 * 5)
        with tiles(e) as i:
            for p in (0, 1):
                e.wait_ge(k.x_tile, i * 2 + (done0 + p - 1))
                ln_turn_pe(e, k, i * 2 + (at0 + p), p, 4 * p)
            for p in (0, 1):
                e.wait_ge(k.xt_sb, i * 2 + (at0 + p + 1 + CREDIT))
                pe_.done(mm(e, bank[:, 4 * p + 1, 0:E + E * R], [(k.xT[p][:, kb], ga[:, kb]) for kb in range(KB)]))
            for p in (0, 1):
                mm(e, bank[:, 4 * p + 2, 0:D], [(k.xT[p][:, kb], wt[:, kb]) for kb in range(KB)], stop=False)
                dve_.wait(e, i, p, "xa")
                pe_.done(e.transpose(bank[:, 4 * p + 3, 0:P], xa[p].rearrange("p e r -> p (e r)"), k.ident[:, :]))
            for p in (0, 1):
                act_.wait(e, i, p, "xaT")
                pe_.done(mm(e, bank[:, 4 * p + 2, 0:D], [(xaT[p], lb)], start=False))

    return dict(sp=sp, pool=pool, dve=dve, act=act, pe=pe)



def retention(k, l):
    H, HD = 2, 128
    at0, done0 = 8 * l, LOADED + 8 * l
    A = Arena(k.arena_buf, 16200)
    W = Arena(k.late[:, 4100:6900], 2800)
    wh = W.take(H, HD)
    wg, wo = W.take(KB, D), W.take(KB, D)
    gam, bet = W.take(D), W.take(D)
    dn = W.take(H, SEQ)
    cs = [A.take(KB, P) for _ in (0, 1)]
    qs = [A.take(H, P) for _ in (0, 1)]
    kd = [A.take(2 * H, 2, SEQ) for _ in (0, 1)]
    V, WR = A.take(NT, D), A.take(NT, D)
    am = A.take(H, SEQ)
    abd = A.take(H, 2, SEQ)
    yn = [A.take(D) for _ in (0, 1)]
    yT = [A.take(KB, P) for _ in (0, 1)]
    ld = k.sem("r4_ld")
    masks0 = k.count_masks(1)
    pl_ = Stages(k.sem("r4_pool"), "cs")
    pe_ = Stages(k.sem("r4_pe"), "qk", "vw", "s")
    dve_ = Stages(k.sem("r4_dve"), "kd", "vw")
    act_ = Stages(k.sem("r4_act"), "q")
    one = k.sem("r4_scores")
    pe2 = Stages(k.sem("r4_pe2"), "o", "turn", "y")
    dve2 = Stages(k.sem("r4_dve2"), "var", "yn")
    act2 = Stages(k.sem("r4_act2"), "yT")
    pl2 = Stages(k.sem("r4_pool2"), "rstd")
    SB_ = 3
    g = k.dram

    def sp(e):
        for dst, src in ((wh, g["r4_wh"]), (wg, g["r4_wg"]), (wo, g["r4_wo"]), (dn, g["r4_decay"]),
                         (gam, g["r4_gamma"].partition_broadcast(P)), (bet, g["r4_beta"].partition_broadcast(P))):
            e.dma_start(dst, src).then_inc(ld, 16)

    def pool(e):
        e.memset(abd, 0.0).then_inc(k.masks, 1)
        with tiles(e) as i:
            for p in (0, 1):
                ln_rstd_pool(e, k, i * 2 + (at0 + p), p)
            for p in (0, 1):
                t = i * 2 + p
                e.wait_ge(k.xt_ps, i * 2 + (at0 + p + 1 + CREDIT))
                pl_.done(e.tensor_copy(cs[p], k.CTXT[:, :, bass.ds(t * P, P)]))
        with tiles(e) as i:
            for p in (0, 1):
                dve2.wait(e, i, p, "var")
                pl2.done(e.tensor_tensor(k.rstd[p][:, :], k.ve[p][:, :], k.half[:, :], ALU.pow))

    def dve(e):
        ch = k.chain(e, "dve")
        e.wait_ge(ld, 16 * 6)

        def body(i, ahead):
            for p in (0, 1):
                pe_.wait(e, i, p, "qk")
                dve_.done(e.tensor_copy(kd[p], bc(k.bank[:, 4 * p + 2, 0:2 * P]
                                                  .rearrange("p (c s) -> p c s", s=SEQ), 2, 2)))
            ahead()
            for p in (0, 1):
                t = i * 2 + p
                pe_.wait(e, i, p, "vw")
                e.tensor_copy(V[:, bass.ds(t, 1)].rearrange("p a d -> p (a d)"), k.bank[:, 4 * p, 0:D])
                dve_.done(e.tensor_scalar(WR[:, bass.ds(t, 1)].rearrange("p a d -> p (a d)"),
                                          k.bank[:, 4 * p, D:2 * D], 0.0, None, ALU.max))

        ln_pair_dve(e, k, ch, at0, 0)
        pairs_ahead(ch, 2 * 2, lambda i: ln_pair_dve(e, k, ch, at0, i), body)
        e.wait_ge(one, 1)
        s = k.bank[:, SB_, 0:H * SEQ].rearrange("p (h s) -> p h s", h=H)
        ch.step(e.scalar_tensor_tensor(am, s, float(HD) ** -0.5, dn, ALU.mult, ALU.mult))
        ch.step(e.scalar_tensor_tensor(am, am, -1.0, am, ALU.mult, ALU.max))
        e.wait_ge(k.masks, masks0 + 1)
        e.tensor_scalar(abd[0:64, :, 0], am[0:64], 1.0, None, ALU.max)
        e.tensor_scalar(abd[64:128, :, 1], am[64:128], 1.0, None, ALU.max).then_inc(one, 1)
        with ch.loop(NT // 2, 2 * (2 + 3)) as i:
            for p in (0, 1):
                pe2.wait(e, i, p, "o")
                ch.step_fixed(e.bn_stats(k.st[p][:, :], k.bank[:, 4 * p, 0:D]))
                ch.step(e.bn_aggr(k.mv[p][:, :], k.st[p][:, :]))
                dve2.done(e.tensor_scalar(k.ve[p][:, :], k.mv[p][:, 1:2], GN_EPS, None, ALU.add))
            for p in (0, 1):
                t = i * 2 + p
                pl2.wait(e, i, p, "rstd")
                ch.step(e.tensor_scalar(yn[p], k.bank[:, 4 * p, 0:D], k.mv[p][:, 0:1], k.rstd[p][:, 0:1],
                                        ALU.subtract, ALU.mult))
                ch.step(e.tensor_tensor(yn[p], yn[p], gam, ALU.mult))
                ch.step(e.tensor_tensor(yn[p], yn[p], bet, ALU.add))
                dve2.done(e.tensor_tensor(yn[p], yn[p], WR[:, bass.ds(t, 1)].rearrange("p a d -> p (a d)"), ALU.mult))
            for p in (0, 1):
                t = i * 2 + p
                pe2.wait(e, i, p, "y")
                e.tensor_tensor(k.X[:, t, :], k.X[:, t, :], k.bank[:, 4 * p + 2, 0:D], ALU.add)\
                    .then_inc(k.x_tile, 1)

    def act(e):
        with tiles(e) as i:
            for p in (0, 1):
                ln_copy_act(e, k, i * 2 + (at0 + p), k.xT[p][:, :, :], 4 * p)
            for p in (0, 1):
                pe_.wait(e, i, p, "qk")
                act_.done(e.copy(qs[p], k.bank[:, 4 * p + 1, 0:2 * P].rearrange("p (h m) -> p h m", h=H)))
        with tiles(e) as i:
            for p in (0, 1):
                pe2.wait(e, i, p, "turn")
                act2.done(e.copy(yT[p], k.bank[:, 4 * p + 1, 0:D].rearrange("p (k m) -> p k m", k=KB)))

    def pe(e):
        bank = k.bank
        e.wait_ge(ld, 16 * 6)
        S = bank[:, SB_, 0:H * SEQ]
        e.matmul(S, k.zeros[:, 0:P], k.zeros[:, 0:H * SEQ], start=True, stop=False)
        with tiles(e) as i:
            for p in (0, 1):
                ln_turn_pe(e, k, i * 2 + (at0 + p), p, 4 * p)
            for p in (0, 1):
                t = i * 2 + p
                e.wait_ge(k.xt_sb, i * 2 + (at0 + p + 1 + CREDIT))
                for h in range(H):
                    e.matmul(bank[:, 4 * p + 1, h * P:(h + 1) * P], wh[:, h], k.xT[p][:, h], start=True, stop=True)
                for h in range(H):
                    ins = e.matmul(bank[:, 4 * p + 2, h * P:(h + 1) * P], wh[:, h],
                                   k.CTXT[:, h, bass.ds(t * P, P)], start=True, stop=True)
                pe_.done(ins)
            for p in (0, 1):
                pl_.wait(e, i, p, "cs")
                for h in range(H):
                    e.matmul(bank[:, 4 * p, h * P:(h + 1) * P], cs[p][:, h], wh[:, h], start=True, stop=True)
                pe_.done(mm(e, bank[:, 4 * p, D:2 * D], [(k.xT[p][:, kb], wg[:, kb]) for kb in range(KB)]))
            for p in (0, 1):
                dve_.wait(e, i, p, "vw")
                act_.wait(e, i, p, "q")
                for h in range(H):
                    for b in (0, 1):
                        ins = e.matmul(bank[:, SB_, h * SEQ:(h + 1) * SEQ],
                                       kd[p][:, 2 * h + b].rearrange("p c s -> p (c s)"),
                                       qs[p][:, h, b * SEQ:(b + 1) * SEQ], start=False, stop=False)
                pe_.done(ins)
        e.matmul(S, k.zeros[:, 0:P], k.zeros[:, 0:H * SEQ], start=False, stop=True).then_inc(one, 1)
        e.wait_ge(one, 2)

        def outs(i):
            for p in (0, 1):
                for h in range(H):
                    ins = e.matmul(bank[:, 4 * p, h * P:(h + 1) * P], abd[:, h].rearrange("p b s -> p (b s)"),
                                   V[:, bass.ds(i * 2 + p, 1), h * P:(h + 1) * P].rearrange("p a d -> p (a d)"),
                                   start=True, stop=True)
                pe2.done(ins)

        def project(i):
            for p in (0, 1):
                dve2.wait(e, i, p, "yn")
                for kb in range(KB):
                    ins = e.transpose(bank[:, 4 * p + 1, kb * P:(kb + 1) * P], yn[p][:, kb * P:(kb + 1) * P],
                                      k.ident[:, :])
                pe2.done(ins)
            for p in (0, 1):
                act2.wait(e, i, p, "yT")
                e.wait_ge(k.x_tile, i * 2 + (done0 + p - 1))
                pe2.done(mm(e, bank[:, 4 * p + 2, 0:D], [(yT[p][:, kb], wo[:, kb]) for kb in range(KB)]))

        outs(0)
        with e.Fori(0, NT // 2 - 1) as i:
            project(i)
            outs(i + 1)
        project(NT // 2 - 1)

    return dict(sp=sp, pool=pool, dve=dve, act=act, pe=pe)


def decay_masks(heads, n):
    gam = np.float32(1.0) - np.float32(2.0) ** (np.float32(-5.0) - np.arange(heads, dtype=np.float32))
    idx = np.arange(n, dtype=np.float32)
    expo = idx[None, :] - idx[:, None]
    d = np.where(expo[None] <= 0, gam[:, None, None].astype(np.float64) ** expo[None], 0.0)
    d = d / np.sqrt(d.sum(axis=-1))[:, None, :]
    return d.astype(np.float32).transpose(2, 0, 1)



def feature_attention(k, l):
    G = 8
    GT = P // G
    masks0 = k.count_masks(6)
    N = 2 * GT
    R = 32
    AHEAD = 3
    at0, done0 = 8 * l, LOADED + 8 * l
    A = Arena(k.arena_buf, 16200)
    cr = k.late[:, 0:NT * D].rearrange("p (t d) -> p t d", d=D)
    m16 = A.take(GT)
    m32 = A.take(R // G, R)
    cm = A.take(GT, D)
    cv = [A.take(KB, GT, R) for _ in (0, 1)]
    nm = [A.take(2) for _ in range(4)]
    sm = [A.take(2) for _ in range(4)]
    ri = [A.take(2) for _ in range(4)]
    pr = [A.take(2, D) for _ in range(4)]
    pT = [A.take(2, D) for _ in (0, 1)]
    ld, cm_ok, cv_ok, s_ps, mx, ex, rs, pn, pt_ps, pt_sb, y_ps = \
        [k.sem("f6_" + n) for n in ("ld", "cm", "cv", "s_ps", "mx", "ex", "rs", "pn", "pt_ps", "pt_sb", "y_ps")]

    def sp(e):
        e.wait_ge(k.x_tile, LOADED + 8 * min(l, 4))
        e.dma_start(cr, k.dram["ctx"].rearrange("(t p) d -> p t d", p=P)).then_inc(ld, 16)

    def pool(e):
        e.memset(m16, float(G) ** -0.5).then_inc(k.masks, 1)
        e.memset(m32, 1.0).then_inc(k.masks, 1)
        e.wait_ge(k.masks, masks0 + 2)
        e.affine_select(out=m16, in_=m16, compare_op=ALU.is_ge, fill=0.0, base=0,
                        pattern=[[-G, GT]], channel_multiplier=1).then_inc(k.masks, 1)
        e.affine_select(out=m32, in_=m32, compare_op=ALU.is_ge, fill=0.0, base=0,
                        pattern=[[-G, R // G], [1, R]], channel_multiplier=0).then_inc(k.masks, 1)
        e.wait_ge(k.masks, masks0 + 4)
        e.affine_select(out=m16, in_=m16, compare_op=ALU.is_ge, fill=0.0, base=G - 1,
                        pattern=[[G, GT]], channel_multiplier=-1).then_inc(k.masks, 1)
        e.affine_select(out=m32, in_=m32, compare_op=ALU.is_ge, fill=0.0, base=G - 1,
                        pattern=[[G, R // G], [-1, R]], channel_multiplier=0).then_inc(k.masks, 1)
        e.wait_ge(k.masks, masks0 + 6)

        def spread(t, p, g):
            e.tensor_tensor(cv[p][:, :, g], k.CTXT[:, :, bass.ds(t * P + g * G // R * R, R)],
                            bc(m32[:, g % (R // G)], 1, KB), ALU.mult).then_inc(cv_ok, 1)

        ln_rstd_pool(e, k, at0, 0)
        for g in range(GT):
            spread(0, 0, g)

        def pair(i, last):
            for n in range(N):
                e.wait_ge(rs, i * N + (n + 1))
                e.tensor_tensor(pr[n % 4], pr[n % 4], bc(ri[n % 4], 2, D), ALU.mult).then_inc(pn, 1)
                if not (last and n >= GT):
                    spread(i * 2 + (n + GT) // GT, (n // GT + 1) % 2, n % GT)
                if n == 2:
                    ln_rstd_pool(e, k, i * 2 + (at0 + 1), 1)
                if n == GT + 2 and not last:
                    ln_rstd_pool(e, k, i * 2 + (at0 + 2), 0)

        with e.Fori(0, NT // 2 - 1) as i:
            pair(i, False)
        pair(NT // 2 - 1, True)

    def dve(e):
        ch = k.chain(e, "dve")

        def top(i, n):
            e.wait_ge(s_ps, i * N + (n + 1))
            e.tensor_reduce(nm[n % 4], k.bank[:, n % 4, :].rearrange("p (b d) -> p b d", d=D), AX.X, ALU.max,
                            negate=True).then_inc(mx, 1)

        def invert(i, n):
            e.wait_ge(ex, i * N + (n + 2))
            e.reciprocal(ri[n % 4], sm[n % 4]).then_inc(rs, 1)

        def turned(i, n):
            e.wait_ge(pt_ps, i * N + (n + 1))
            e.tensor_copy(pT[n % 2], k.bank[:, 4 + n % 2, :].rearrange("p (n m) -> p n m", n=2)).then_inc(pt_sb, 1)

        def add(i, p):
            e.wait_ge(y_ps, i * 2 + (p + 1))
            x = k.X[:, bass.ds(i * 2 + p, 1)].rearrange("p a d -> p (a d)")
            e.tensor_tensor(x, x, k.bank[:, 6 + p, 0:D], ALU.add).then_inc(k.x_tile, 1)

        ln_stats_dve(e, k, ch, 0, 0)
        ln_norm_dve(e, k, at0, 0, 0).then_inc(k.ln_out, 1)
        for n in range(AHEAD):
            top(0, n)
        invert(0, 0)

        def pair(i, last):
            for n in range(N):
                if not last or n + 1 < N:
                    invert(i, n + 1)
                if not last or n + AHEAD < N:
                    top(i, n + AHEAD)
                turned(i, n)
                if n == 2:
                    ln_stats_dve(e, k, ch, i * 2 + 1, 1)
                if n == 4:
                    ln_norm_dve(e, k, i * 2 + (at0 + 1), i * 2 + 1, 1).then_inc(k.ln_out, 1)
                if not last and n == GT + 2:
                    ln_stats_dve(e, k, ch, i * 2 + 2, 0)
                if not last and n == GT + 4:
                    ln_norm_dve(e, k, i * 2 + (at0 + 2), i * 2 + 2, 0).then_inc(k.ln_out, 1)
                if n == GT + 1:
                    add(i, 0)
            add(i, 1)

        with ch.loop(NT // 2 - 1, 4) as i:
            pair(i, False)
        pair(NT // 2 - 1, True)

    def act(e):
        e.sem_inc(k.xt_sb, NT)
        e.sem_inc(ex, 1)
        e.wait_ge(ld, 16)
        e.wait_ge(k.masks, masks0 + 6)

        def spread(t, g):
            e.activation(cm[:, g], cr[:, bass.ds(t, 1)].rearrange("p a d -> p (a d)"), ACT.Identity,
                         scale=m16[:, g:g + 1]).then_inc(cm_ok, 1)

        for g in range(GT):
            spread(0, g)

        def pair(i, last):
            for n in range(N):
                e.wait_ge(mx, i * N + (n + 1))
                for b in (0, 1):
                    ins = e.activation(pr[n % 4][:, b], k.bank[:, n % 4, b * D:(b + 1) * D], ACT.Exp,
                                       bias=nm[n % 4][:, b:b + 1], accum_out=sm[n % 4][:, b:b + 1])
                ins.then_inc(ex, 1)
                if not (last and n >= GT):
                    spread(i * 2 + (n + GT) // GT, n % GT)

        with e.Fori(0, NT // 2 - 1) as i:
            pair(i, False)
        pair(NT // 2 - 1, True)

    def pe(e):
        bank = k.bank

        def scores(i, n, first=False):
            p, g = n // GT % 2, n % GT
            if g == 0:
                e.wait_ge(k.ln_out, i * 2 + (at0 + n // GT + 1))
            e.wait_ge(cm_ok, i * N + (n + 1))
            if not first:
                e.wait_ge(ex, i * N + (n - 2))
            for b in (0, 1):
                ins = e.matmul(bank[:, n % 4, b * D:(b + 1) * D], k.xs[p][:, b * P:(b + 1) * P], cm[:, g],
                               start=True, stop=True)
            ins.then_inc(s_ps, 1)
            if g == GT - 1:
                e.wait_ge(s_ps, i * N + (n + 1))
                e.sem_inc(k.xt_ps, 1)

        def turn(i, n):
            e.wait_ge(pn, i * N + (n + 1))
            for c in (0, 1):
                for b in (0, 1):
                    ins = e.transpose(bank[:, 4 + n % 2, (2 * c + b) * P:(2 * c + b + 1) * P],
                                      pr[n % 4][:, b, c * P:(c + 1) * P], k.ident[:, :])
            ins.then_inc(pt_ps, 1)

        def values(i, n):
            p, g = n // GT, n % GT
            if g == 0:
                e.wait_ge(k.x_tile, i * 2 + (done0 + p - 1))
            e.wait_ge(cv_ok, i * N + (n + 1))
            e.wait_ge(pt_sb, i * N + (n + 1))
            r = g * G // R * R
            for c in (0, 1):
                ins = e.matmul(bank[r:r + R, 6 + p, 0:D], cv[p][:, c, g], pT[n % 2][:, c],
                               start=g * G % R == 0 and c == 0, stop=(g + 1) * G % R == 0 and c == 1)
            if g == GT - 1:
                ins.then_inc(y_ps, 1)

        for n in range(AHEAD):
            scores(0, n, first=True)

        def pair(i, last):
            for n in range(N):
                if not last or n + AHEAD < N:
                    scores(i, n + AHEAD)
                turn(i, n)
                if n > 0:
                    values(i, n - 1)
            values(i, N - 1)

        with e.Fori(0, NT // 2 - 1) as i:
            pair(i, False)
        pair(NT // 2 - 1, True)

    return dict(sp=sp, pool=pool, dve=dve, act=act, pe=pe)



def peer_mlp(k, l):
    I = 1024
    K, TOP, NE = PEER_KEYS, PEER_TOP, PEER_EXPERTS
    RD = 64
    IB, EB = I // P, NE // P
    POOLED = 3
    MINE = TOP - POOLED
    at0, done0 = 8 * l, LOADED + 8 * l
    A = Arena(k.arena_buf, 16200)
    W = Arena(k.early, 13200)
    wq = W.take(KB, P)
    keys = W.take(2, K)
    wgu = W.take(KB, 4, 512)
    de, ue, dn = W.take(KB, NE), W.take(EB, D), W.take(IB, D)
    XP = k.CTXT.ap().rearrange("p k t -> p (k t)").rearrange("p (u d) -> p u d", d=D)
    qT = A.take(T)
    rs = A.take(2, NT // 2, 2 * K)
    rr = [A.take(2, K) for _ in (0, 1)]
    xt = [A.take(KB, P) for _ in (0, 1)]
    m0, m1, m8 = [[A.take(TOP) for _ in (0, 1)] for _ in range(3)]
    i0, i1, pk = [[A.take(TOP, dt=U32) for _ in (0, 1)] for _ in range(3)]
    f0, f1, fk = [[A.take(TOP) for _ in (0, 1)] for _ in range(3)]
    alls, alli = A.take(TOP, TOP), A.take(TOP, TOP)
    oh = A.take(TOP, TOP * TOP)
    neg = [A.take(1) for _ in (0, 1)]
    sm, ri = [[A.take(1) for _ in (0, 1)] for _ in range(2)]
    w8 = [A.take(TOP) for _ in (0, 1)]
    ix = [A.take(TOP) for _ in (0, 1)]
    iota64, iota512 = A.take(TOP * TOP), A.take(NE)
    wd = [A.take(NE) for _ in (0, 1)]
    wp = [A.take(NE) for _ in (0, 1)]
    td, tp = A.take(MINE, NE), A.take(NE)
    hs = [A.take(3, 512) for _ in (0, 1)]
    hT = [A.take(3, 4, P) for _ in (0, 1)]
    names = ("ld", "xd", "xp", "q_ps", "q_sb", "r_sb", "xt", "f_ps", "silu", "h", "t_ps", "t_act",
             "t_dve", "o_ps", "top", "exp", "ix", "wp", "st")
    S = {n: k.sem("p7_" + n) for n in names}
    g = k.dram
    masks0 = k.count_masks(2)
    OUT = 7

    def rows(j, h):
        return g["out"].rearrange("(j p h) d -> j h p d", p=P, h=2)[bass.ds(j, 1), h].rearrange("j p d -> p (j d)")

    def sp(e):
        e.wait_ge(k.x_tile, LOADED + 8 * min(l, 6))
        for dst, src in ((wq, g["p7_q"]), (keys, g["p7_keys"]), (wgu, g["p7_gu"]), (de, g["p7_de"]),
                         (ue, g["p7_ue"]), (dn, g["p7_dn"])):
            e.dma_start(dst, src).then_inc(S["ld"], 16)
        e.wait_ge(k.x_tile, LOADED + 8 * l)
        e.dma_start(g["xd"].rearrange("(t p) d -> p t d", p=P), k.X[:, :, :]).then_inc(S["xd"], 16)
        e.wait_ge(S["xd"], 16)
        e.dma_start(XP.rearrange("p (j h) d -> p j h d", h=2), g["xd"].rearrange("(j p h) d -> p j h d", p=P, h=2))\
            .then_inc(S["xp"], 16)
        with tiles(e) as i:
            for p in (0, 1):
                u = i * 2 + p
                e.wait_ge(k.x_tile, u + (done0 + 1))
                e.dma_start(rows(i, p), XP[:, bass.ds(u, 1)].rearrange("p u d -> p (u d)")).then_inc(S["st"], 16)
        e.wait_ge(S["st"], 16 * NT)

    def pool(e):
        e.iota(iota64, pattern=[[1, TOP * TOP]], base=0, channel_multiplier=0, allow_small_or_imprecise_dtypes=True)\
            .then_inc(k.masks, 1)
        e.iota(iota512, pattern=[[1, NE]], base=0, channel_multiplier=0, allow_small_or_imprecise_dtypes=True)\
            .then_inc(k.masks, 1)
        e.wait_ge(k.masks, masks0 + 2)
        with tiles(e) as i:
            for p in (0, 1):
                ln_rstd_pool(e, k, i * 2 + (at0 + p), p)

        def tile_x(u, p, first=False):
            if not first:
                e.wait_ge(S["f_ps"], u * 3 - 3)
            if isinstance(u, int):
                src = k.XNT[:, :, (u // 2) * 2 * P:(u // 2 + 1) * 2 * P].rearrange("p k (m h) -> p k m h", h=2)[:, :, :, p]
            else:
                src = k.XNT[:, :, bass.ds((u - p) * P, 2 * P)].rearrange("p k (m h) -> p k m h", h=2)[:, :, :, p]
            e.tensor_copy(xt[p], src).then_inc(S["xt"], 1)

        ch = Chain(e, S["wp"], k.passed)
        per = 2 * POOLED - 1

        def hot(u, p):
            e.wait_ge(S["ix"], u + 1)
            ch.apart()
            for n in range(POOLED):
                c = TOP - POOLED + n
                (ch.step_fixed if n == 0 else ch.step)(e.tensor_scalar(wp[p] if n == 0 else tp, iota512, ix[p][:, c:c + 1], w8[p][:, c:c + 1],
                                        ALU.is_equal, ALU.mult))
                if n > 0:
                    ch.step_fixed(e.tensor_tensor(wp[p], wp[p], tp, ALU.add))

        e.wait_ge(k.xt_sb, at0 + NT + CREDIT)
        tile_x(0, 0, True)
        tile_x(1, 1, True)
        hot(0, 0)
        hot(1, 1)
        with ch.loop(NT // 2 - 1, 2 * per) as i:
            for p in (0, 1):
                u = i * 2 + (p + 2)
                tile_x(u, p)
                e.wait_ge(S["h"], u * 3 - 3)
                hot(u, p)

    def dve(e):
        ch = k.chain(e, "dve")
        ln_tiles_dve(e, k, ch, at0)
        e.wait_ge(S["q_ps"], 4)
        for b in (0, 1):
            ch.step(e.tensor_copy(rs[:, b], k.bank[:, 2 + b, :].rearrange("p (u c) -> p u c", c=2 * K)))
        e.sem_inc(S["r_sb"], 1)
        e.wait_ge(k.masks, masks0 + 2)
        e.wait_ge(S["xp"], 16)

        def route(j, p):
            ch.step_fixed(e.tensor_copy(rr[p].rearrange("p t c -> p (t c)"), rs[:, p, bass.ds(j, 1)].rearrange("p u c -> p (u c)")))
            ch.mark(e.max(m0[p], rr[p][:, 0]))
            ch.step_fixed(e.max(m1[p], rr[p][:, 1]))
            ch.mark(e.max_index(i0[p], m0[p], rr[p][:, 0]))
            ch.step(e.max_index(i1[p], m1[p], rr[p][:, 1]))
            ch.mark(e.tensor_copy(f0[p], i0[p]))
            ch.mark(e.tensor_copy(f1[p], i1[p]))
            ch.step(e.tensor_tensor(alls, bc(m0[p], 2, TOP), bc(m1[p], 1, TOP), ALU.add))
            ch.mark(e.tensor_scalar(f0[p], f0[p], float(K), None, ALU.mult))
            ch.step_fixed(e.max(m8[p], alls.rearrange("p i j -> p (i j)")))
            ch.step(e.max_index(pk[p], m8[p], alls.rearrange("p i j -> p (i j)")))
            e.tensor_scalar(neg[p], m8[p][:, 0:1], -1.0, None, ALU.mult).then_inc(S["top"], 1)
            ch.step(e.tensor_tensor(alli, bc(f0[p], 2, TOP), bc(f1[p], 1, TOP), ALU.add))
            ch.step(e.tensor_copy(fk[p], pk[p]))

        ROUTE = 13

        def weigh(u, p):
            ch.step(e.tensor_tensor(oh, bc(fk[p], 2, TOP * TOP), bc(iota64, 1, TOP), ALU.is_equal))
            ch.step(e.tensor_tensor(oh, oh, bc(alli.rearrange("p i j -> p (i j)"), 1, TOP), ALU.mult))
            ch.step(e.tensor_reduce(ix[p], oh, AX.X, ALU.add))
            e.wait_ge(S["exp"], u + 1)
            ch.step(e.reciprocal(ri[p], sm[p]))
            ch.mark(e.tensor_scalar(w8[p], w8[p], ri[p], None, ALU.mult))
            e.tensor_scalar(ix[p], ix[p], NE - 1.0, None, ALU.min).then_inc(S["ix"], 1)

        WEIGH = 5

        def hot(p):
            for c in range(MINE):
                ch.mark(e.tensor_scalar(td[:, c], iota512, ix[p][:, c:c + 1], w8[p][:, c:c + 1],
                                        ALU.is_equal, ALU.mult))

        def hot_sum(p):
            ch.wait()
            ch.step(e.tensor_tensor(td[:, 0:2], td[:, 0:2], td[:, 2:4], ALU.add))
            ch.step(e.tensor_tensor(td[:, 0], td[:, 0], td[:, 1], ALU.add))
            ch.mark(e.tensor_tensor(wd[p], td[:, 0], td[:, 4], ALU.add))

        HOT = MINE + 3

        def product(u, p, c):
            e.wait_ge(S["silu"], u * 3 + (c + 1))
            if c < 2:
                e.tensor_tensor(hs[p][:, c], hs[p][:, c], k.bank[:, 2 * c + 1, :], ALU.mult).then_inc(S["h"], 1)
            else:
                e.wait_ge(S["wp"], (u + 1) * (2 * POOLED - 1))
                ch.wait()
                ch.step(e.tensor_tensor(wd[p], wd[p], wp[p], ALU.add))
                e.tensor_tensor(hs[p][:, c], hs[p][:, c], wd[p], ALU.mult).then_inc(S["h"], 1)

        def turned(u, p, c):
            e.wait_ge(S["t_ps"], u * 3 + (c + 1))
            e.tensor_copy(hT[p][:, c], k.bank[:, 5 + c % 2, :].rearrange("p (b m) -> p b m", m=P))\
                .then_inc(S["t_dve"], 1)

        def add(u):
            e.wait_ge(S["o_ps"], u + 1)
            x = XP[:, bass.ds(u, 1)].rearrange("p u d -> p (u d)")
            e.tensor_tensor(x, x, k.bank[:, OUT, 0:D], ALU.add).then_inc(k.x_tile, 1)

        for u in (0, 1):
            route(0, u)
            weigh(u, u)
        e.wait_ge(S["ix"], 2)
        hot(0)
        hot_sum(0)
        for c in range(3):
            product(0, 0, c)

        def unit(u, p, routes):
            turned(u, p, 0)
            e.wait_ge(S["ix"], u + 2)
            hot(1 - p)
            product(u + 1, 1 - p, 0)
            hot_sum(1 - p)
            product(u + 1, 1 - p, 1)
            turned(u, p, 2)
            product(u + 1, 1 - p, 2)
            if routes is not None:
                route(routes, p)
                weigh(u + 2, p)
            add(u)

        with ch.loop(NT // 2 - 1, 2 * (ROUTE + WEIGH + HOT + 1)) as i:
            for p in (0, 1):
                unit(i * 2 + p, p, i + 1)
        unit(NT - 2, 0, None)
        turned(NT - 1, 1, 0)
        turned(NT - 1, 1, 2)
        add(NT - 1)

    def act(e):
        with tiles(e) as i:
            for p in (0, 1):
                t = i * 2 + p
                ln_copy_act(e, k, i * 2 + (at0 + p), k.XNT[:, :, bass.ds(t * P, P)], p)
        for n in (0, 1):
            e.wait_ge(S["q_ps"], n + 1)
            e.copy(qT[:, 512 * n:512 * n + 512], k.bank[:, n, :]).then_inc(S["q_sb"], 1)

        def exp(u, p):
            e.wait_ge(S["top"], u + 1)
            e.activation(w8[p], m8[p], ACT.Exp, bias=neg[p], accum_out=sm[p]).then_inc(S["exp"], 1)

        def silu(u, p, c):
            e.wait_ge(S["f_ps"], u * 3 + (c + 1))
            e.activation(hs[p][:, c], k.bank[:, 2 * c, :], ACT.Silu).then_inc(S["silu"], 1)

        def turned(u, p):
            e.wait_ge(S["t_ps"], u * 3 + 2)
            e.copy(hT[p][:, 1], k.bank[:, 6, :].rearrange("p (b m) -> p b m", m=P)).then_inc(S["t_act"], 1)

        exp(0, 0)
        exp(1, 1)
        for c in range(3):
            silu(0, 0, c)

        def unit(u, p, routes):
            silu(u + 1, 1 - p, 0)
            turned(u, p)
            silu(u + 1, 1 - p, 1)
            silu(u + 1, 1 - p, 2)
            if routes:
                e.wait_ge(S["wp"], (u + 1) * (2 * POOLED - 1))
                exp(u + 2, p)

        with e.Fori(0, NT // 2 - 1) as i:
            for p in (0, 1):
                unit(i * 2 + p, p, True)
        unit(NT - 2, 0, False)
        turned(NT - 1, 1)

    def pe(e):
        bank = k.bank
        with tiles(e) as i:
            for p in (0, 1):
                ln_turn_pe(e, k, i * 2 + (at0 + p), p, p)
        e.wait_ge(S["ld"], 16 * 6)
        e.wait_ge(k.xt_sb, at0 + NT + CREDIT)
        for n in (0, 1):
            mm(e, bank[:, n, :], [(wq[:, kb], k.XNT[:, kb, 512 * n:512 * n + 512]) for kb in range(KB)])\
                .then_inc(S["q_ps"], 1)
        e.wait_ge(S["q_sb"], 2)
        for u in range(NT):
            r = slice(RD * (u % 2), RD * (u % 2) + RD)
            for side in (0, 1):
                at = u // 2 * 2 * K + side * K
                q = side * (T // 2) + u // 2 * P
                ins = e.matmul(bank[:, 2 + u % 2, at:at + K], qT[r, q:q + P], keys[r, side], start=True, stop=True)
            if u >= NT - 2:
                ins.then_inc(S["q_ps"], 1)

        def front(u, p, c):
            if c == 0:
                e.wait_ge(S["xt"], u + 1)
            if not isinstance(u, int) or u > 0:
                e.wait_ge(S["h"] if c < 2 else S["silu"], u * 3 + (c - 2))
            elif c == 1:
                e.wait_ge(S["r_sb"], 1)
            if c < 2:
                for b in (0, 1):
                    ins = mm(e, bank[:, 2 * c + b, :], [(xt[p][:, kb], wgu[:, kb, 2 * c + b]) for kb in range(KB)])
            else:
                ins = mm(e, bank[:, 4, :], [(xt[p][:, kb], de[:, kb]) for kb in range(KB)])
            ins.then_inc(S["f_ps"], 1)

        def turn(u, p, c, first=False):
            e.wait_ge(S["h"], u * 3 + (c + 1))
            if c == 0:
                if not first:
                    e.wait_ge(S["t_dve"], u * 2)
            elif c == 1:
                if not first:
                    e.wait_ge(S["t_act"], u)
            else:
                e.wait_ge(S["t_dve"], u * 2 + 1)
            for b in range(4):
                ins = e.transpose(bank[:, 5 + c % 2, b * P:(b + 1) * P], hs[p][:, c, b * P:(b + 1) * P], k.ident[:, :])
            ins.then_inc(S["t_ps"], 1)

        def down(u, p, first=False):
            e.wait_ge(S["t_act"], u + 1)
            e.wait_ge(S["t_dve"], u * 2 + 2)
            if not first:
                e.wait_ge(k.x_tile, u + done0)
            mm(e, bank[:, OUT, 0:D], [(hT[p][:, b // 4, b % 4], dn[:, b] if b < IB else ue[:, b - IB])
                                      for b in range(IB + EB)]).then_inc(S["o_ps"], 1)

        for c in range(3):
            front(0, 0, c)

        def unit(u, p, first=False):
            for c in range(3):
                turn(u, p, c, first)
                front(u + 1, 1 - p, c)
            down(u, p, first)

        unit(0, 0, True)
        with e.Fori(0, NT // 2 - 1) as i:
            for p in (1, 0):
                unit(i * 2 + (2 - p), p)
        for c in range(3):
            turn(NT - 1, 1, c)
        down(NT - 1, 1)

    return dict(sp=sp, pool=pool, dve=dve, act=act, pe=pe, stores=True)


MAKERS = {
    0: attention_qdq,
    1: lambda k, l: experts(k, l, 176, 176, (88, 88), k.early[:, 3600:9600], True, "m1"),
    2: attention_wide,
    3: lora_mixture,
    4: retention,
    5: lambda k, l: experts(k, l, 704, 352, (128,) * 5 + (64,), k.early[:, 0:13200], False, "m5"),
    6: feature_attention,
    7: peer_mlp,
}


def later_layers(a, rows, cols):
    def packed(w):
        return w.reshape(w.shape[0], -1, P, w.shape[2]).transpose(0, 2, 1, 3)

    g = {}
    g["m1_gate"] = rows(a["L0_ffn_gate_weight"].T)
    g["sh_g"], g["sh_u"] = rows(a["L0_ffn_sh_gate_w"].T), rows(a["L0_ffn_sh_up_w"].T)
    g["sh_d"] = a["L0_ffn_sh_down_w"].T
    g["m1_gu"] = packed(np.concatenate([a["L0_ffn_gate_w"], a["L0_ffn_up_w"]], axis=1).transpose(0, 2, 1))
    g["m1_d"] = a["L0_ffn_down_w"].transpose(0, 2, 1)
    g["m5_gate"] = rows(a["L2_ffn_Wg"])
    g["m5_gu"] = packed(np.concatenate([a["L2_ffn_W1"], a["L2_ffn_W3"]], axis=2))
    g["m5_d"] = a["L2_ffn_W2"]
    heads = [a["L1_xattn_" + n].reshape(KB, P, 16, P).transpose(2, 1, 0, 3) for n in ("Wq", "Wk", "Wv")]
    g["a2_qkv"] = np.stack(heads, axis=2)
    g["a2_o"] = a["L1_xattn_Wo"].reshape(16, P, D)
    lora_a = a["L1_ffn_lora_A"].reshape(-1, D)
    g["l3_ga"] = rows(np.concatenate([a["L1_ffn_gate_w"], lora_a], axis=0).T)
    g["l3_w"] = rows(a["L1_ffn_W"].T)
    g["l3_b"] = a["L1_ffn_lora_B"].transpose(0, 2, 1).reshape(-1, D)
    g["l3_bias"], g["l3_gb"] = a["L1_ffn_b"], a["L1_ffn_gate_b"]
    g["r4_wh"] = a["L2_xattn_Wh"].transpose(1, 0, 2)
    g["r4_wg"], g["r4_wo"] = rows(a["L2_xattn_wg_w"]), rows(a["L2_xattn_wo_w"])
    g["r4_gamma"], g["r4_beta"] = a["L2_xattn_gn_gamma"], a["L2_xattn_gn_beta"]
    g["r4_decay"] = np.tile(decay_masks(2, SEQ), (2, 1, 1))
    g["p7_q"] = rows(a["L3_ffn_W_q"])
    g["p7_keys"] = np.tile(a["L3_ffn_keys"].transpose(1, 0, 2), (2, 1, 1))
    gu = np.stack([a["L3_ffn_gate_w"].reshape(D, 2, 512), a["L3_ffn_up_w"].reshape(D, 2, 512)], axis=2)
    g["p7_gu"] = gu.reshape(KB, P, 4, 512).transpose(1, 0, 2, 3)
    g["p7_de"], g["p7_ue"], g["p7_dn"] = rows(a["L3_ffn_down_embed"].T), rows(a["L3_ffn_up_embed"]), rows(a["L3_ffn_down_w"])
    return g


def program(nc, dram, out, which=range(LAYERS)):
    with ExitStack() as ctx:
        dram = dict(dram, xg=nc.dram_tensor("xg", (SLOTS * P, D), F32, kind="Internal").ap(),
                    yg=nc.dram_tensor("yg", (SLOTS * P, D), F32, kind="Internal").ap(),
                    xd=nc.dram_tensor("xd", (T, D), F32, kind="Internal").ap(), out=out)
        k = shared(nc, ctx, dram)
        stages = [constants(k)] + [MAKERS[l](k, n) for n, l in enumerate(which)]
        out_st = k.sem("out_st")
        block = ctx.enter_context(nc.Block())

        def run(e, who):
            for n, s in enumerate(stages):
                if n > 0 and who != "sp":
                    e.wait_ge(k.x_tile, LOADED + 8 * (n - 1))
                if who in s:
                    s[who](e)

        @block.sync
        def _(e):
            e.dma_start(k.X[:, :, :], dram["x"].rearrange("(t p) d -> p t d", p=P)).then_inc(k.x_tile, 16)
            e.dma_start(k.CTXT[:, :, :], dram["ctxT"]).then_inc(k.ctx_ld, 16)
            run(e, "sp")
            if "stores" in stages[-1]:
                return
            e.wait_ge(k.x_tile, LOADED + 8 * (len(stages) - 1))
            e.dma_start(out.rearrange("(t p) d -> p t d", p=P), k.X[:, :, :]).then_inc(out_st, 16)
            e.wait_ge(out_st, 16)

        @block.gpsimd
        def _(e):
            run(e, "pool")

        @block.vector
        def _(e):
            run(e, "dve")

        @block.scalar
        def _(e):
            run(e, "act")

        @block.tensor
        def _(e):
            run(e, "pe")


def laid_out(a):
    def rows(w):
        return w.reshape(-1, P, w.shape[1]).transpose(1, 0, 2)

    def cols(v):
        return v.reshape(-1, P).T

    ctx = a["ctx_2048"].reshape(T, D)
    g = dict(x=a["x"].reshape(T, D), ctx=ctx, ctxT=rows(ctx.T))
    g["wq"], g["wp"] = rows(a["L0_xattn_wq"]), rows(a["L0_xattn_wp"])
    g["wkT"], g["wvT"] = rows(a["L0_xattn_wkv"][:D].T), rows(a["L0_xattn_wkv"][D:].T)
    g["bqk"] = np.concatenate([cols(a["L0_xattn_bq"]), cols(a["L0_xattn_bkv"][:D])], axis=1)
    g["bv"], g["bp"] = a["L0_xattn_bkv"][D:], a["L0_xattn_bp"]
    g.update(later_layers(a, rows, cols))
    return g


def kernel(**inputs):
    import concourse.bacc as bacc
    from concourse.bass_utils import run_bass_kernel_spmd

    a = {n: np.asarray(v) for n, v in inputs.items()}
    nc = bacc.Bacc("TRN2", target_bir_lowering=False, num_devices=1)
    arrays, dram = {}, {}
    for name, v in laid_out(a).items():
        arrays[name] = np.ascontiguousarray(v)
        dram[name] = nc.dram_tensor(name, v.shape, mybir.dt.from_np(v.dtype), kind="ExternalInput").ap()
    out = nc.dram_tensor("out", (T, D), F32, kind="ExternalOutput").ap()
    program(nc, dram, out)
    r = run_bass_kernel_spmd(nc, [arrays], core_ids=[0])
    return r.results[0]["out"].reshape(a["x"].shape)
```
